# Optimizing a Trainium2 kernel written in Bass

```python
import numpy as np
import jax
import jax.numpy as jnp

def _softmax(x, axis=-1):
    return jax.nn.softmax(x, axis=axis)

def _gelu(x):
    return jax.nn.gelu(x, approximate=True)

def _silu(x):
    return jax.nn.silu(x)

def _sigmoid(x):
    return jax.nn.sigmoid(x)

def _layernorm(x, axis=-1, eps=1e-05):
    m = jnp.mean(x, axis=axis, keepdims=True)
    v = jnp.var(x, axis=axis, keepdims=True)
    return (x - m) / jnp.sqrt(v + eps)

def _scatter_add(tgt, idx, src, axis=0):
    return tgt.at[idx].add(src)

def _segment_sum(src, seg, n):
    return jax.ops.segment_sum(src, seg, n)
kernel_name = 'mk_hybrid_d1_jaxref_r8_36b89c'

def setup_inputs(seed: int=0):
    np.random.seed(seed)
    _w = jnp.asarray

    def _L0_attn_a_setup():
        import jax, jax.numpy as jnp
        import numpy as np
        import math
        H = 16
        EPS = 1e-05
        key = jax.random.key(seed)
        ks = jax.random.split(key, 4)
        B, T, D = (2, 256, 128)
        s = 1.0 / math.sqrt(D)
        return {'x': jax.random.normal(ks[0], (B, T, D), dtype=jnp.float32), 'ln_g': jnp.ones((D,), jnp.float32), 'ln_b': jnp.zeros((D,), jnp.float32), 'Wq': jax.random.normal(ks[1], (D, D), jnp.float32) * s, 'bq': jnp.zeros((D,), jnp.float32), 'Wk': jax.random.normal(ks[2], (D, D), jnp.float32) * s, 'bk': jnp.zeros((D,), jnp.float32), 'Wv': jax.random.normal(ks[3], (D, D), jnp.float32) * s, 'bv': jnp.zeros((D,), jnp.float32)}
    _L0_attn_a_in = _L0_attn_a_setup()

    def _L0_attn_b_setup():
        import jax, jax.numpy as jnp
        import numpy as np
        B, S, D = (2, 256, 128)
        H = 16
        DK = 128
        DV = 128
        EPS = 1e-05
        key = jax.random.key(seed)
        k1, k2, k3, k4 = jax.random.split(key, 4)
        x = jax.random.normal(k1, (B, S, D), dtype=jnp.float32)
        Wq = jax.random.normal(k2, (DK, D), dtype=jnp.float32) * 0.02
        Wk = jax.random.normal(k3, (DK, D), dtype=jnp.float32) * 0.02
        Wv = jax.random.normal(k4, (DV, D), dtype=jnp.float32) * 0.02
        return {'x': x, 'Wq': Wq, 'Wk': Wk, 'Wv': Wv}
    _L0_attn_b_in = _L0_attn_b_setup()

    def _L0_ffn_setup():
        import jax, jax.numpy as jnp
        import numpy as np
        DIM = 128
        DEPTH = 6
        HEADS = 16
        DIM_HEAD = 64
        WINDOW = 32
        INNER = HEADS * DIM_HEAD
        DIM_INNER = int(DIM * 4 * 2 / 3)
        QK_SCALE = 8.0

        def shift_tokens(t):
            a, s = jnp.split(t, 2, -1)
            s = jnp.pad(s, ((0, 0), (1, 0), (0, 0)))[:, :-1]
            return jnp.concatenate([a, s], -1)

        def l2norm(t):
            return t / jnp.maximum(jnp.linalg.norm(t, axis=-1, keepdims=True), 1e-12)

        def rotate_half(x):
            x1, x2 = jnp.split(x, 2, -1)
            return jnp.concatenate([-x2, x1], -1)

        def rotary_tables(n):
            half = jnp.arange(0, DIM_HEAD, 2, dtype=jnp.float32)
            inv_freq = 1.0 / 10000.0 ** (half / DIM_HEAD)
            t = jnp.arange(n, dtype=jnp.float32)
            freqs = t[:, None] * inv_freq[None, :]
            freqs = jnp.concatenate([freqs, freqs], -1)
            base_scale = (half + 0.4 * DIM_HEAD) / (1.4 * DIM_HEAD)
            power = (t - n // 2) / (WINDOW // 2)
            scale = base_scale[None, :] ** power[:, None]
            scale = jnp.concatenate([scale, scale], -1)
            return (freqs, scale)

        def local_attention(q, k, v):
            b, h, n, d = q.shape
            w = WINDOW
            nw = n // w
            bq = q.reshape(b, h, nw, w, d)
            bk = k.reshape(b, h, nw, w, d)
            bv = v.reshape(b, h, nw, w, d)

            def look(t):
                p = jnp.pad(t, ((0, 0), (0, 0), (1, 0), (0, 0), (0, 0)))
                return jnp.concatenate([p[:, :, :nw], p[:, :, 1:]], axis=3)
            bk2, bv2 = (look(bk), look(bv))
            seq = jnp.arange(n).reshape(nw, w)
            seq_p = jnp.pad(seq, ((1, 0), (0, 0)), constant_values=-1)
            jt = jnp.concatenate([seq_p[:nw], seq_p[1:]], axis=1)
            it = seq[:, :, None]
            jb = jt[:, None, :]
            mask = (it < jb) | (it > jb + w) | (jb == -1)
            sim = jnp.einsum('bhwie,bhwje->bhwij', bq, bk2) * QK_SCALE
            sim = jnp.where(mask, -jnp.finfo(sim.dtype).max, sim)
            attn = jax.nn.softmax(sim, -1)
            out = jnp.einsum('bhwij,bhwje->bhwie', attn, bv2)
            return out.reshape(b, h, n, d)

        def attn_layer(x, Wqkv, qs, ksc, Wo):
            b, n, _ = x.shape
            qkv = x @ Wqkv
            q, k, v = jnp.split(qkv, 3, -1)
            sh = lambda t: t.reshape(b, n, HEADS, DIM_HEAD).transpose(0, 2, 1, 3)
            q, k, v = (sh(q), sh(k), sh(v))
            q = l2norm(q) * qs
            k = l2norm(k) * ksc
            freqs, scale = rotary_tables(n)
            cos, sin = (jnp.cos(freqs), jnp.sin(freqs))
            q = q * cos * scale + rotate_half(q) * sin * scale
            inv = 1.0 / scale
            k = k * cos * inv + rotate_half(k) * sin * inv
            out = local_attention(q, k, v)
            out = out.transpose(0, 2, 1, 3).reshape(b, n, INNER)
            return out @ Wo

        def ffn_layer(x, g, bln, W1, b1, W2, b2):
            mu = x.mean(-1, keepdims=True)
            var = ((x - mu) ** 2).mean(-1, keepdims=True)
            xn = (x - mu) / jnp.sqrt(var + 1e-05) * g + bln
            hg = xn @ W1 + b1
            a, gate = jnp.split(hg, 2, -1)
            return a * jax.nn.gelu(gate, approximate=False) @ W2 + b2
        key = jax.random.key(seed)
        ks = jax.random.split(key, 8)
        B, N = (2, 256)
        init = lambda k, shape: jax.random.normal(k, shape, jnp.float32) * 0.02
        return {'x': jax.random.normal(ks[0], (B, N, DIM), jnp.float32), 'Wqkv': init(ks[1], (DEPTH, DIM, 3 * INNER)), 'q_scale': jnp.ones((DEPTH, DIM_HEAD), jnp.float32), 'k_scale': jnp.ones((DEPTH, DIM_HEAD), jnp.float32), 'Wo': init(ks[2], (DEPTH, INNER, DIM)), 'ln_g': jnp.ones((DEPTH, DIM), jnp.float32), 'ln_b': jnp.zeros((DEPTH, DIM), jnp.float32), 'W1': init(ks[3], (DEPTH, DIM, 2 * DIM_INNER)), 'b1': jnp.zeros((DEPTH, 2 * DIM_INNER), jnp.float32), 'W2': init(ks[4], (DEPTH, DIM_INNER, DIM)), 'b2': jnp.zeros((DEPTH, DIM), jnp.float32)}
    _L0_ffn_in = _L0_ffn_setup()
    _d = {'L0_attn_a_x': _L0_attn_a_in['x'], 'L0_attn_a_ln_g': _L0_attn_a_in['ln_g'], 'L0_attn_a_ln_b': _L0_attn_a_in['ln_b'], 'L0_attn_a_Wq': _L0_attn_a_in['Wq'], 'L0_attn_a_bq': _L0_attn_a_in['bq'], 'L0_attn_a_Wk': _L0_attn_a_in['Wk'], 'L0_attn_a_bk': _L0_attn_a_in['bk'], 'L0_attn_a_Wv': _L0_attn_a_in['Wv'], 'L0_attn_a_bv': _L0_attn_a_in['bv'], 'L0_attn_b_Wq': _L0_attn_b_in['Wq'], 'L0_attn_b_Wk': _L0_attn_b_in['Wk'], 'L0_attn_b_Wv': _L0_attn_b_in['Wv'], 'L0_ffn_Wqkv': _L0_ffn_in['Wqkv'], 'L0_ffn_q_scale': _L0_ffn_in['q_scale'], 'L0_ffn_k_scale': _L0_ffn_in['k_scale'], 'L0_ffn_Wo': _L0_ffn_in['Wo'], 'L0_ffn_ln_g': _L0_ffn_in['ln_g'], 'L0_ffn_ln_b': _L0_ffn_in['ln_b'], 'L0_ffn_W1': _L0_ffn_in['W1'], 'L0_ffn_b1': _L0_ffn_in['b1'], 'L0_ffn_W2': _L0_ffn_in['W2'], 'L0_ffn_b2': _L0_ffn_in['b2']}
    _x0 = _d['L0_attn_a_x']
    _d['L0_attn_a_x'] = jax.random.normal(jax.random.fold_in(jax.random.key(seed), 1), (4, 512, 128), dtype=_x0.dtype)
    del _x0
    return _d

def reference(L0_attn_a_x, L0_attn_a_ln_g, L0_attn_a_ln_b, L0_attn_a_Wq, L0_attn_a_bq, L0_attn_a_Wk, L0_attn_a_bk, L0_attn_a_Wv, L0_attn_a_bv, L0_attn_b_Wq, L0_attn_b_Wk, L0_attn_b_Wv, L0_ffn_Wqkv, L0_ffn_q_scale, L0_ffn_k_scale, L0_ffn_Wo, L0_ffn_ln_g, L0_ffn_ln_b, L0_ffn_W1, L0_ffn_b1, L0_ffn_W2, L0_ffn_b2):

    def _L0_attn_a_ref(x, ln_g, ln_b, Wq, bq, Wk, bk, Wv, bv):
        import jax, jax.numpy as jnp
        import numpy as np
        import math
        H = 16
        EPS = 1e-05
        B, T, D = x.shape
        mu = jnp.mean(x, axis=-1, keepdims=True)
        var = jnp.mean(jnp.square(x - mu), axis=-1, keepdims=True)
        xn = (x - mu) * jax.lax.rsqrt(var + EPS) * ln_g + ln_b
        q = (xn @ Wq + bq).reshape(B, T, H, D // H)
        k = (xn @ Wk + bk).reshape(B, T, H, D // H)
        v = (xn @ Wv + bv).reshape(B, T, H, D // H)
        scale = 1.0 / math.sqrt(D // H)
        attn = jnp.einsum('bnhd,bmhd->bnmh', q, k) * scale
        w = jax.nn.softmax(attn, axis=2)
        y = jnp.einsum('bnmh,bmhd->bnhd', w, v).reshape(B, T, D)
        return y

    def _L0_attn_b_ref(x, Wq, Wk, Wv):
        import jax, jax.numpy as jnp
        import numpy as np
        B, S, D = (2, 256, 128)
        H = 16
        DK = 128
        DV = 128
        EPS = 1e-05
        b, s, d = x.shape
        dkh = DK // H
        dvh = DV // H
        Q = (x @ Wq.T).reshape(H, b, s, dkh)
        K = (x @ Wk.T).reshape(H, b, s, dkh)
        V = (x @ Wv.T).reshape(H, b, s, dvh)
        scores = jnp.einsum('hbqd,hbkd->hbqk', Q, K)
        atten = jax.nn.softmax(scores, axis=-1)
        out = jnp.einsum('hbqk,hbkd->hbqd', atten, V).reshape(b, s, -1)
        y = out + x
        mu = jnp.mean(y, axis=(1, 2), keepdims=True)
        var = jnp.var(y, axis=(1, 2), keepdims=True)
        return (y - mu) / jnp.sqrt(var + EPS)

    def _L0_ffn_ref(x, Wqkv, q_scale, k_scale, Wo, ln_g, ln_b, W1, b1, W2, b2):
        import jax, jax.numpy as jnp
        import numpy as np
        DIM = 128
        DEPTH = 6
        HEADS = 16
        DIM_HEAD = 64
        WINDOW = 32
        INNER = HEADS * DIM_HEAD
        DIM_INNER = int(DIM * 4 * 2 / 3)
        QK_SCALE = 8.0

        def shift_tokens(t):
            a, s = jnp.split(t, 2, -1)
            s = jnp.pad(s, ((0, 0), (1, 0), (0, 0)))[:, :-1]
            return jnp.concatenate([a, s], -1)

        def l2norm(t):
            return t / jnp.maximum(jnp.linalg.norm(t, axis=-1, keepdims=True), 1e-12)

        def rotate_half(x):
            x1, x2 = jnp.split(x, 2, -1)
            return jnp.concatenate([-x2, x1], -1)

        def rotary_tables(n):
            half = jnp.arange(0, DIM_HEAD, 2, dtype=jnp.float32)
            inv_freq = 1.0 / 10000.0 ** (half / DIM_HEAD)
            t = jnp.arange(n, dtype=jnp.float32)
            freqs = t[:, None] * inv_freq[None, :]
            freqs = jnp.concatenate([freqs, freqs], -1)
            base_scale = (half + 0.4 * DIM_HEAD) / (1.4 * DIM_HEAD)
            power = (t - n // 2) / (WINDOW // 2)
            scale = base_scale[None, :] ** power[:, None]
            scale = jnp.concatenate([scale, scale], -1)
            return (freqs, scale)

        def local_attention(q, k, v):
            b, h, n, d = q.shape
            w = WINDOW
            nw = n // w
            bq = q.reshape(b, h, nw, w, d)
            bk = k.reshape(b, h, nw, w, d)
            bv = v.reshape(b, h, nw, w, d)

            def look(t):
                p = jnp.pad(t, ((0, 0), (0, 0), (1, 0), (0, 0), (0, 0)))
                return jnp.concatenate([p[:, :, :nw], p[:, :, 1:]], axis=3)
            bk2, bv2 = (look(bk), look(bv))
            seq = jnp.arange(n).reshape(nw, w)
            seq_p = jnp.pad(seq, ((1, 0), (0, 0)), constant_values=-1)
            jt = jnp.concatenate([seq_p[:nw], seq_p[1:]], axis=1)
            it = seq[:, :, None]
            jb = jt[:, None, :]
            mask = (it < jb) | (it > jb + w) | (jb == -1)
            sim = jnp.einsum('bhwie,bhwje->bhwij', bq, bk2) * QK_SCALE
            sim = jnp.where(mask, -jnp.finfo(sim.dtype).max, sim)
            attn = jax.nn.softmax(sim, -1)
            out = jnp.einsum('bhwij,bhwje->bhwie', attn, bv2)
            return out.reshape(b, h, n, d)

        def attn_layer(x, Wqkv, qs, ksc, Wo):
            b, n, _ = x.shape
            qkv = x @ Wqkv
            q, k, v = jnp.split(qkv, 3, -1)
            sh = lambda t: t.reshape(b, n, HEADS, DIM_HEAD).transpose(0, 2, 1, 3)
            q, k, v = (sh(q), sh(k), sh(v))
            q = l2norm(q) * qs
            k = l2norm(k) * ksc
            freqs, scale = rotary_tables(n)
            cos, sin = (jnp.cos(freqs), jnp.sin(freqs))
            q = q * cos * scale + rotate_half(q) * sin * scale
            inv = 1.0 / scale
            k = k * cos * inv + rotate_half(k) * sin * inv
            out = local_attention(q, k, v)
            out = out.transpose(0, 2, 1, 3).reshape(b, n, INNER)
            return out @ Wo

        def ffn_layer(x, g, bln, W1, b1, W2, b2):
            mu = x.mean(-1, keepdims=True)
            var = ((x - mu) ** 2).mean(-1, keepdims=True)
            xn = (x - mu) / jnp.sqrt(var + 1e-05) * g + bln
            hg = xn @ W1 + b1
            a, gate = jnp.split(hg, 2, -1)
            return a * jax.nn.gelu(gate, approximate=False) @ W2 + b2
        for i in range(DEPTH):
            x = attn_layer(shift_tokens(x), Wqkv[i], q_scale[i], k_scale[i], Wo[i]) + x
            x = ffn_layer(shift_tokens(x), ln_g[i], ln_b[i], W1[i], b1[i], W2[i], b2[i]) + x
        return x
    x = L0_attn_a_x
    x = x + _L0_attn_a_ref(_layernorm(x, axis=-1), L0_attn_a_ln_g, L0_attn_a_ln_b, L0_attn_a_Wq, L0_attn_a_bq, L0_attn_a_Wk, L0_attn_a_bk, L0_attn_a_Wv, L0_attn_a_bv)
    x = x + _L0_ffn_ref(_layernorm(x, axis=-1), L0_ffn_Wqkv, L0_ffn_q_scale, L0_ffn_k_scale, L0_ffn_Wo, L0_ffn_ln_g, L0_ffn_ln_b, L0_ffn_W1, L0_ffn_b1, L0_ffn_W2, L0_ffn_b2)
    x = x + _L0_attn_b_ref(_layernorm(x, axis=-1), L0_attn_b_Wq, L0_attn_b_Wk, L0_attn_b_Wv)
    x = x + _L0_ffn_ref(_layernorm(x, axis=-1), L0_ffn_Wqkv, L0_ffn_q_scale, L0_ffn_k_scale, L0_ffn_Wo, L0_ffn_ln_g, L0_ffn_ln_b, L0_ffn_W1, L0_ffn_b1, L0_ffn_W2, L0_ffn_b2)
    return x

_drawn_inputs = setup_inputs


def setup_inputs(seed=0):
    import zlib

    import numpy as np

    out = dict(_drawn_inputs(seed))
    spreads = {'L0_attn_a_ln_g': (1.0, 0.2),
     'L0_attn_a_ln_b': (0.0, 0.1),
     'L0_attn_a_bq': (0.0, 0.639),
     'L0_attn_a_bk': (0.0, 0.8),
     'L0_attn_a_bv': (0.0, 0.1),
     'L0_ffn_q_scale': (1.0, 0.6),
     'L0_ffn_k_scale': (1.0, 0.6),
     'L0_ffn_ln_g': (1.0, 0.6),
     'L0_ffn_ln_b': (0.0, 0.8),
     'L0_ffn_b1': (0.0, 0.653),
     'L0_ffn_b2': (0.0, 0.1)}
    factors = {'L0_attn_b_Wq': 8.0, 'L0_attn_b_Wk': 8.0, 'L0_attn_b_Wv': 8.0}
    for name, (base, spread) in spreads.items():
        noise = np.random.default_rng([zlib.crc32(name.encode()), seed]).standard_normal(out[name].shape)
        drawn = base * np.exp(spread * noise) if base else spread * noise
        out[name] = jnp.asarray(drawn.astype(out[name].dtype))
    for name, factor in factors.items():
        out[name] = (out[name] * factor).astype(out[name].dtype)
    return out
```

```python
import numpy as np

import concourse.bass as bass
from concourse import mybir
from contextlib import ExitStack

F32 = mybir.dt.float32
BF16 = mybir.dt.bfloat16
I32 = mybir.dt.int32
ALU = mybir.AluOpType
ACT = mybir.ActivationFunctionType
AX = mybir.AxisListType.X

B, T, D = 4, 512, 128
N = B * T
EPS = 1e-5
NH, DH = 16, 8
QB4 = T // 128
PARTS = 3
Q_PARTS = (0, 0, 1, 1, 0, 2)
K_PARTS = (0, 1, 0, 1, 2, 0)
SROWS = DH * len(Q_PARTS)
LAYERS = 6
LH, LD = 16, 64
INNER = LH * LD
WIN = 32
FF = int(D * 4 * 2 / 3)
FT = (FF + 127) // 128
FR = [min(128, FF - 128 * t) for t in range(FT)]
HP = LH // 2
STEPS = LAYERS * B
BLK = T // 128
QK_SCALE = 8.0
MASKED = -1e37
MAGIC = 1597463007.0
NEWTON = 3
RN = 3 + 3 * NEWTON
P_B1A, P_B1G, P_B2, P_G, P_B, NPAR = 0, FT, 2 * FT, 2 * FT + 1, 2 * FT + 2, 2 * FT + 3
LN_PART = [0, 3 * B + STEPS]
LN_STACK = [3 * B, 3 * B + STEPS + 2 * B]
VEC_LOADS = 5 + 2 * FT + 3 + 2
LINKS = [23, 42]


def host_constants():
    half = np.arange(0, LD, 2, dtype=np.float32)
    inv_freq = (np.float32(1.0) / np.float32(10000.0) ** (half / np.float32(LD))).astype(np.float32)
    t = np.arange(T, dtype=np.float32)
    freqs = (t[:, None] * inv_freq[None, :]).astype(np.float32)
    freqs = np.concatenate([freqs, freqs], -1)
    base = ((half + np.float32(0.4 * LD)) / np.float32(1.4 * LD)).astype(np.float32)
    power = ((t - T // 2) / (WIN // 2)).astype(np.float32)
    scale = (base[None, :] ** power[:, None]).astype(np.float32)
    scale = np.concatenate([scale, scale], -1)
    cos, sin = np.cos(freqs), np.sin(freqs)
    sign = np.where(np.arange(LD) < LD // 2, 1.0, -1.0).astype(np.float32)
    inv = (np.float32(1.0) / scale).astype(np.float32)
    kinds = [cos * scale, np.roll(sin * scale, LD // 2, 1) * sign, cos * inv, np.roll(sin * inv, LD // 2, 1) * sign]
    kinds[0], kinds[1] = kinds[0] * np.float32(QK_SCALE), kinds[1] * np.float32(QK_SCALE)
    rot = np.stack(kinds, 1).reshape(BLK, 128, 4, LD).transpose(1, 0, 2, 3).reshape(128, -1)
    r = np.arange(128)[:, None] % WIN
    k = np.arange(2 * WIN)[None, :]
    bad = (r > k) | (k > r + WIN)
    mask = np.stack([bad, bad | ((k < WIN) & (np.arange(128)[:, None] < WIN))], 1).reshape(128, -1) * MASKED
    row, col = np.arange(128)[:, None], np.arange(128)[None, :]
    sel = (row == 32 * (col // 32) + DH).astype(np.float32)
    return np.concatenate([rot, mask, np.eye(128), sel], 1).astype(np.float32)


C_ROT, C_MASK = 0, BLK * 4 * LD
C_ID = C_MASK + 2 * 2 * WIN
C_SEL = C_ID + 128
NCON = C_SEL + 128


def hybrid_kernel(nc, a, out, scr_parts, scr_max, scr_att):
    with ExitStack() as ctx:
        def sb(name, shape, dt=F32):
            return ctx.enter_context(nc.sbuf_tensor(name, shape, dt))

        def sem(name):
            return ctx.enter_context(nc.semaphore(name))

        X = sb("X", [128, N])
        Y = sb("Y", [128, N])
        CON = sb("CON", [128, NCON])
        IDB = sb("IDB", [128, 128], BF16)
        MASKB = sb("MASKB", [128, 2, 2 * WIN], BF16)
        AVG = sb("AVG", [128, 128])
        IDF = CON[:, C_ID:C_ID + 128]
        SELB = CON[:, C_SEL:C_SEL + 128]
        ROT = CON[:, C_ROT:C_MASK].rearrange("p (n k f) -> p n k f", n=BLK, k=4)
        XF = sb("XF", [128, T])
        XC = sb("XC", [128, T])
        XQ = sb("XQ", [128, T])
        XN = sb("XN", [128, T])
        NV = sb("NV", [128, T])
        NY = sb("NY", [128, T])
        NA = sb("NA", [128, T])
        WA = sb("WA", [128, 3, 128])
        WB = sb("WB", [128, 3, 128])
        VEC = sb("VEC", [128, 4])
        BVB = sb("BVB", [128, 128])
        W = sb("W", [128, 2, 3 * INNER])
        WO = sb("WO", [128, 2, HP, D])
        W1 = sb("W1", [128, 2 * FF])
        W2 = sb("W2", [128, FT, D])
        PARL = sb("PARL", [128, LAYERS, NPAR])
        PAR = sb("PAR", [128, NPAR])
        QSC = sb("QSC", [128, LAYERS, 2, LD])
        TAB = sb("TAB", [128, BLK, 4, LD])
        XS = sb("XS", [128, WIN + T])
        XSW = sb("XSW", [128, BLK, 2, 128])
        ROTB = sb("ROTB", [128, 6 * T])
        SQ = ROTB[:, 0:2 * T].rearrange("p (r t) -> p r t", r=2)
        T1 = ROTB[:, 2 * T:4 * T].rearrange("p (r t) -> p r t", r=2)
        T2 = ROTB[:, 4 * T:6 * T].rearrange("p (r t) -> p r t", r=2)
        SS = sb("SS", [128, 32])
        SV = sb("SV", [128, 32])
        SY = sb("SY", [128, 32])
        SA = sb("SA", [128, 32])
        QN = sb("QN", [128, 4, T])
        QT = sb("QT", [128, HP, 128])
        KT = sb("KT", [128, BLK, HP, WIN + 128])
        VT = sb("VT", [128, 2, 4, T])
        PB = sb("PB", [128, HP, 2, LD])
        PT = sb("PT", [128, HP, 128])
        ON = sb("ON", [128, HP, 2, LD])
        OT = sb("OT", [128, HP, T])
        MXS = sb("MXS", [128, 2, HP])
        SMS = sb("SMS", [128, 2, HP])
        RSS = sb("RSS", [128, 2, HP])
        GG = sb("GG", [128, FT, T])
        HT = sb("HT", [128, FT, T])
        QS = KT[:, :, :, :].rearrange("p n h t -> p (n h t)")[:, 0:NH * T // 2].bitcast(BF16)\
            .rearrange("p (h t) -> p h t", h=NH)
        KS = OT[:, :, :].rearrange("p h t -> p (h t)").bitcast(BF16).rearrange("p (h t) -> p h t", h=NH)
        STG = VT[:, :, :, :].rearrange("p r v t -> p (r v t)").bitcast(BF16).rearrange("p (c t) -> p c t", c=NH)
        PX = VT
        VA = ROTB[:, 0:4 * T].rearrange("p (h k d) -> p h k d", h=NH, k=QB4)
        PTS = GG[:, :, :].rearrange("p a t -> p (a t)").bitcast(BF16).rearrange("p (a t) -> p a t", t=T)
        QF, KF, RES = HT[:, 0, :], HT[:, 1, :], HT[:, 2, :]
        OS = QN
        RC = PB[:, 0:4, :, :].rearrange("p h s d -> p (h s d)")
        ATT = PT[:, 0:4, :].rearrange("p h t -> p (h t)")
        MX = SS
        MXA = sb("MXA", [128, 64])
        MT = sb("MT", [32, PARTS, 128], BF16)
        MR = sb("MR", [32, 128])
        STAT = sb("STAT", [128, 8])
        XL = QN

        def bank(name):
            return ctx.enter_context(nc.psum_tensor(name, [128, T], F32))

        R4 = ctx.enter_context(nc.psum_tensor("R4", [128, 4, T], F32))
        QBK = [R4[:, 0, :], R4[:, 1, :]]
        TB = [R4[:, 2, :], R4[:, 3, :]]
        SB = [bank("S0"), bank("S1")]
        MB = [bank("M0"), bank("M1")]
        OB = SB

        con_loaded = sem("con_loaded")
        mats_loaded = sem("mats_loaded")
        vecs_loaded = sem("vecs_loaded")
        consts = sem("consts")
        parl_clear = sem("parl_clear")
        x_loaded = sem("x_loaded")
        x_t = sem("x_t")
        x_ready = sem("x_ready")
        wb_t = sem("wb_t")
        wb_ready = sem("wb_ready")
        ln_in = sem("ln_in")
        ln_mean = sem("ln_mean")
        ln_xc = sem("ln_xc")
        ln_sq = sem("ln_sq")
        ln_var = sem("ln_var")
        ln_step = sem("ln_step")
        zeros = sem("zeros")
        y_ready = sem("y_ready")
        xn_aff = sem("xn_aff")
        xn_part = sem("xn_part")
        q_mm = sem("q_mm")
        k_mm = sem("k_mm")
        vp_mm = sem("vp_mm")
        chain = sem("chain")
        va_clear = sem("va_clear")
        va_ready = sem("va_ready")
        parts_ready = sem("parts_ready")
        scr_written = sem("scr_written")
        qs_loaded = sem("qs_loaded")
        qs_ordered = sem("qs_ordered")
        smax_mm = sem("smax_mm")
        max_red = sem("max_red")
        nm_ready = sem("nm_ready")
        nm_t = sem("nm_t")
        mt_ready = sem("mt_ready")
        m_written = sem("m_written")
        m_loaded = sem("m_loaded")
        st_mm = sem("st_mm")
        exp_p = sem("exp_p")
        pv_mm = sem("pv_mm")
        os_ready = sem("os_ready")
        den_mm = sem("den_mm")
        on_part = sem("on_part")
        att_written = sem("att_written")
        att_loaded = sem("att_loaded")
        stat_in = sem("stat_in")
        stat_mm = sem("stat_mm")
        wqkv_loaded = sem("wqkv_loaded")
        wo_loaded = sem("wo_loaded")
        w12_loaded = sem("w12_loaded")
        xs_copied = sem("xs_copied")
        xs_ready = sem("xs_ready")
        tab_ready = sem("tab_ready")
        par_ready = sem("par_ready")
        qk_mm = sem("qk_mm")
        sq_done = sem("sq_done")
        ss_done = sem("ss_done")
        rot_mul = sem("rot_mul")
        rot_add = sem("rot_add")
        rn_step = sem("rn_step")
        qk_norm = sem("qk_norm")
        b_mm = sem("b_mm")
        qt_ready = sem("qt_ready")
        s_mm = sem("s_mm")
        pv_turn = sem("pv_turn")
        max_done = sem("max_done")
        sub_done = sem("sub_done")
        exp_done = sem("exp_done")
        sum_done = sem("sum_done")
        rs_done = sem("rs_done")
        v_mm = sem("v_mm")
        v_ready = sem("v_ready")
        d_mm = sem("d_mm")
        pt_ready = sem("pt_ready")
        e_mm = sem("e_mm")
        on_ready = sem("on_ready")
        g_mm = sem("g_mm")
        ot_ready = sem("ot_ready")
        wo_mm = sem("wo_mm")
        y_attn = sem("y_attn")
        xn_ready = sem("xn_ready")
        gate_mm = sem("gate_mm")
        gelu_done = sem("gelu_done")
        a_mm = sem("a_mm")
        h_ready = sem("h_ready")
        w2_mm = sem("w2_mm")
        o_t = sem("o_t")
        o_ready = sem("o_ready")
        o_stored = sem("o_stored")

        def seen(count):
            return max(count, 0) if isinstance(count, int) else count

        block = ctx.enter_context(nc.Block())

        def batch_cols(t, b):
            return t[:, bass.ds(b * T, T)]

        def rsqrt(v, y, tmp, src, op, const, step, base, y_users=None, y_used=0):
            vec = nc.vector
            vec.tensor_scalar(out=v, in0=src, scalar1=const, scalar2=None, op0=op).then_inc(step, 1)
            vec.wait_ge(step, base + 1)
            vec.tensor_scalar(out=tmp.bitcast(I32), in0=v.bitcast(I32), scalar1=1, scalar2=None,
                              op0=ALU.logical_shift_right).then_inc(step, 1)
            vec.wait_ge(step, base + 2)
            if y_users is not None:
                vec.wait_ge(y_users, y_used)
            vec.tensor_scalar(out=y.bitcast(I32), in0=tmp.bitcast(I32), scalar1=-1.0, scalar2=MAGIC,
                              op0=ALU.mult, op1=ALU.add).then_inc(step, 1)
            for it in range(NEWTON):
                vec.wait_ge(step, base + 3 + 3 * it)
                vec.tensor_tensor(out=tmp, in0=v, in1=y, op=ALU.mult).then_inc(step, 1)
                vec.wait_ge(step, base + 4 + 3 * it)
                vec.scalar_tensor_tensor(out=tmp, in0=tmp, scalar=-0.5, in1=y, op0=ALU.mult, op1=ALU.mult)\
                   .then_inc(step, 1)
                vec.wait_ge(step, base + 5 + 3 * it)
                vec.scalar_tensor_tensor(out=y, in0=tmp, scalar=1.5, in1=y, op0=ALU.add, op1=ALU.mult)\
                   .then_inc(step, 1)
            vec.wait_ge(step, base + RN)

        def ln_center(k):
            nc.vector.wait_ge(ln_mean, k + 1)
            nc.vector.tensor_tensor(out=XC[:, :], in0=XF[:, :], in1=MB[0][:, :], op=ALU.subtract)\
                .then_inc(ln_xc, 1)

        def ln_scale(k, dst, signal):
            nc.vector.wait_ge(ln_var, k + 1)
            rsqrt(NV[:, :], NY[:, :], NA[:, :], MB[1][:, :], ALU.add, EPS, ln_step, RN * k)
            nc.vector.tensor_tensor(out=dst, in0=XC[:, :], in1=NY[:, :], op=ALU.mult).then_inc(signal, 1)

        def ln_mean_mm(k):
            nc.tensor.wait_ge(ln_in, k + 1)
            nc.tensor.matmul(MB[0][:, :], AVG[:, :], XF[:, :], start=True, stop=True).then_inc(ln_mean, 1)

        def ln_var_mm(k):
            nc.tensor.wait_ge(ln_sq, k + 1)
            nc.tensor.matmul(MB[1][:, :], AVG[:, :], XQ[:, :], start=True, stop=True).then_inc(ln_var, 1)

        def ln_square(k):
            nc.scalar.wait_ge(ln_xc, k + 1)
            nc.scalar.activation(XQ[:, :], XC[:, :], ACT.Square).then_inc(ln_sq, 1)

        def part_loop(eng, body):
            with eng.Fori(0, B) as b:
                body(b)

        @block.vector
        def _(dve):
            vec = nc.vector
            dve.wait_ge(con_loaded, 16)
            vec.tensor_copy(IDB[:, :], IDF).then_inc(consts, 1)
            vec.tensor_copy(MASKB[:, :, :], CON[:, C_MASK:C_ID].rearrange("p (m k) -> p m k", m=2))\
               .then_inc(consts, 1)
            vec.memset(AVG[:, :], 1.0 / D).then_inc(consts, 1)

            def part(p):
                def body(b):
                    c = B * p + b
                    count = [0]
                    base = LINKS[0] * c if p == 0 else LINKS[0] * B + LINKS[1] * b

                    def link(ins):
                        count[0] += 1
                        ins.then_inc(chain, 1)
                        dve.wait_ge(chain, base + count[0])

                    xb = batch_cols(X, b)
                    k0 = LN_PART[p] + (3 - p) * b
                    if p == 0:
                        vec.tensor_scalar(out=XF[:, :], in0=xb, scalar1=1.0, scalar2=None, op0=ALU.mult)\
                            .then_inc(ln_in, 1)
                        ln_center(k0)
                        ln_scale(k0, XF[:, :], ln_in)
                        dve.wait_ge(ln_in, k0 + 2)
                        k0 = k0 + 1
                        ln_center(k0)
                        ln_scale(k0, XN[:, :], xn_aff)
                        dve.wait_ge(xn_aff, b + 1)
                        vec.tensor_scalar(out=XN[:, :], in0=XN[:, :], scalar1=VEC[:, 2:3], scalar2=VEC[:, 3:4],
                                          op0=ALU.mult, op1=ALU.add).then_inc(xn_part, 1)
                    else:
                        link(vec.tensor_tensor(out=xb, in0=xb, in1=batch_cols(Y, b), op=ALU.add))
                        vec.tensor_scalar(out=XF[:, :], in0=xb, scalar1=1.0, scalar2=None, op0=ALU.mult)\
                            .then_inc(ln_in, 1)
                        ln_center(k0)
                        ln_scale(k0, XN[:, :], xn_part)
                    dve.wait_ge(q_mm, c + 1)
                    if p == 0:
                        link(vec.tensor_scalar(out=QF, in0=MB[0][:, :], scalar1=VEC[:, 0:1],
                                               scalar2=float(1.0 / np.sqrt(DH)), op0=ALU.add, op1=ALU.mult))
                    else:
                        link(vec.tensor_copy(QF, MB[0][:, :]))
                    dve.wait_ge(k_mm, c + 1)
                    if p == 0:
                        link(vec.tensor_scalar(out=KF, in0=MB[1][:, :], scalar1=VEC[:, 1:2], scalar2=None,
                                               op0=ALU.add))
                    else:
                        link(vec.tensor_copy(KF, MB[1][:, :]))
                    dve.wait_ge(vp_mm, c + 1)
                    dve.wait_ge(va_clear, 2 * p + 2)
                    if p == 0:
                        vec.tensor_tensor(
                            out=VA[:, :, :, 0:DH].rearrange("p h k d -> p k h d"),
                            in0=MB[0][:, :].rearrange("p (k h d) -> p k h d", k=QB4, h=NH),
                            in1=BVB[:, :].rearrange("p (h d) -> p h d", h=NH).unsqueeze(1)
                            .broadcast_to([128, QB4, NH, DH]), op=ALU.add).then_inc(va_ready, 1)
                    else:
                        for j in range(4):
                            for cc in range(4):
                                src = MB[0][32 * j:32 * j + 32, :].rearrange(
                                    "t (n k c d) -> t n k c d", n=4, k=4, c=4)[:, :, :, cc, :]
                                last = vec.tensor_copy(VA[32 * cc:32 * cc + 32, j::4, :, 0:DH], src)
                        last.then_inc(va_ready, 1)
                    for z, f in enumerate((QF, KF)):
                        first = vec.tensor_copy(PTS[:, PARTS * z, :], f)
                        link(first)
                        link(vec.tensor_tensor(out=RES, in0=f, in1=PTS[:, PARTS * z, :], op=ALU.subtract))
                        link(vec.tensor_copy(PTS[:, PARTS * z + 1, :], RES))
                        link(vec.tensor_tensor(out=RES, in0=RES, in1=PTS[:, PARTS * z + 1, :], op=ALU.subtract))
                        vec.tensor_copy(PTS[:, PARTS * z + 2, :], RES).then_inc(parts_ready, 1)
                        dve.wait_ge(parts_ready, 2 * c + z + 1)

                    if p == 1:
                        dve.wait_ge(qs_loaded, 16 * 12 * (c + 1))
                        dve.wait_ge(va_clear, 2 * p + 1)
                        for z, dst in enumerate((QS, KS)):
                            vec.tensor_copy(dst[0:SROWS, :, :].rearrange("r h (c t) -> r h c t", t=32),
                                            STG[64 * z:64 * z + SROWS, :, :].rearrange("r c (h t) -> r h c t", t=32))\
                               .then_inc(qs_ordered, 1)

                    def sums(g):
                        dve.wait_ge(pv_mm, 16 * c + 4 * g + 4)
                        vec.tensor_copy(OS[:, g, :], OB[g % 2][:, :]).then_inc(os_ready, 1)

                    for hh in range(2):
                        for u in range(32 * hh, 32 * hh + 32):
                            dve.wait_ge(smax_mm, 64 * c + u + 1)
                            vec.tensor_reduce(out=MXA[:, u:u + 1], in_=MB[u % 2][:, :], op=ALU.max, axis=AX)\
                               .then_inc(max_red, 1)
                        dve.wait_ge(max_red, 64 * c + 32 * hh + 32)
                        vec.tensor_scalar(out=MX[:, :], in0=MXA[:, 32 * hh:32 * hh + 32], scalar1=-1.0, scalar2=None,
                                          op0=ALU.mult).then_inc(nm_ready, 1)
                        dve.wait_ge(nm_t, 2 * c + hh + 1)
                        if hh == 1:
                            dve.wait_ge(m_written, 16 * (2 * c + 1))
                        mps = MB[0][0:32, 0:128]
                        link(vec.tensor_copy(MT[:, 0, :], mps))
                        link(vec.tensor_tensor(out=MR[:, :], in0=mps, in1=MT[:, 0, :], op=ALU.subtract))
                        link(vec.tensor_copy(MT[:, 1, :], MR[:, :]))
                        link(vec.tensor_tensor(out=MR[:, :], in0=MR[:, :], in1=MT[:, 1, :], op=ALU.subtract))
                        vec.tensor_copy(MT[:, 2, :], MR[:, :]).then_inc(mt_ready, 1)
                        dve.wait_ge(mt_ready, 2 * c + hh + 1)
                    for g in range(4):
                        sums(g)
                    for g in range(4):
                        dve.wait_ge(den_mm, 4 * c + g + 1)
                        link(vec.reciprocal(RC, MB[g % 2][:, :]))
                        vec.tensor_tensor(out=OS[:, g, :], in0=OS[:, g, :], in1=RC, op=ALU.mult)\
                           .then_inc(on_part, 1)
                        dve.wait_ge(on_part, 4 * c + g + 1)
                    dve.wait_ge(att_loaded, 16 * (c + 1))
                    if p == 0:
                        link(vec.tensor_tensor(out=xb, in0=xb, in1=ATT, op=ALU.add))
                    else:
                        link(vec.tensor_tensor(out=XC[:, :], in0=ATT, in1=XN[:, :], op=ALU.add))
                        link(vec.reduce_sum(STAT[:, 0:1], XC[:, :], axis=AX))
                        vec.tensor_scalar(out=STAT[:, 1:2], in0=STAT[:, 0:1], scalar1=1.0 / T, scalar2=None,
                                          op0=ALU.mult).then_inc(stat_in, 1)
                        dve.wait_ge(stat_mm, 2 * b + 1)
                        link(vec.tensor_copy(STAT[:, 2:3], MB[0][:, 0:1]))
                        link(vec.tensor_scalar(out=XC[:, :], in0=XC[:, :], scalar1=STAT[:, 2:3], scalar2=None,
                                               op0=ALU.subtract))
                        link(vec.tensor_tensor(out=XF[:, :], in0=XC[:, :], in1=XC[:, :], op=ALU.mult))
                        link(vec.reduce_sum(STAT[:, 3:4], XF[:, :], axis=AX))
                        vec.tensor_scalar(out=STAT[:, 4:5], in0=STAT[:, 3:4], scalar1=1.0 / T, scalar2=None,
                                          op0=ALU.mult).then_inc(stat_in, 1)
                        dve.wait_ge(stat_mm, 2 * b + 2)
                        rsqrt(STAT[:, 5:6], STAT[:, 6:7], STAT[:, 7:8], MB[0][:, 0:1], ALU.add, EPS, chain,
                              base + count[0])
                        count[0] += RN
                        link(vec.scalar_tensor_tensor(out=xb, in0=XC[:, :], scalar=STAT[:, 6:7], in1=xb,
                                                      op0=ALU.mult, op1=ALU.add))
                    kl = LN_PART[p] + (3 - p) * b + (2 - p)
                    vec.tensor_scalar(out=XF[:, :], in0=xb, scalar1=1.0, scalar2=None, op0=ALU.mult)\
                            .then_inc(ln_in, 1)
                    ln_center(kl)
                    ln_scale(kl, batch_cols(Y, b), y_ready)
                    dve.wait_ge(y_ready, (B + STEPS) * p + b + 1)
                    assert count[0] == LINKS[p], (p, count[0])
                part_loop(dve, body)

            def stack(ph):
                def prep(i, m, done):
                    b = (i % B) * T
                    lo = 1 if m == 0 else 0
                    vec.tensor_scalar(out=XS[0:64, WIN + 128 * m:WIN + 128 * m + 128],
                                      in0=Y[0:64, bass.ds(b + 128 * m, 128)], scalar1=1.0, scalar2=None,
                                      op0=ALU.mult)
                    vec.tensor_copy(XS[64:128, WIN + 128 * m + lo:WIN + 128 * m + 128],
                                    Y[64:128, bass.ds(b + 128 * m + lo - 1, 128 - lo)]).then_inc(xs_copied, 1)
                    dve.wait_ge(xs_copied, done)
                    for v in range(2):
                        lo = WIN + 128 * m - WIN * v
                        last = vec.tensor_copy(XSW[:, m, v, :].rearrange("p (z t) -> p z t", z=2),
                                               XS[:, lo:lo + 128].rearrange("p (z t) -> p z t", z=2)[:, ::-1, :])
                    last.then_inc(xs_ready, 1)

                vec.memset(XS[:, 0:WIN + 1], 0.0).then_inc(zeros, 1)
                vec.memset(KT[:, 0, :, 0:WIN], 0.0).then_inc(zeros, 1)
                vec.memset(XF[64:128, 0:1], 0.0).then_inc(zeros, 1)
                dve.wait_ge(zeros, 3 * ph + 3)
                for m in range(BLK - 1):
                    prep(0, m, (BLK * STEPS + BLK - 1) * ph + m + 1)

                def body(i, cur, prev):
                    for n in range(BLK):
                        has_prev = (cur and n > 0) or (prev and n == 0)
                        G = BLK * STEPS * ph + BLK * i + n
                        GX = (BLK * STEPS + BLK - 1) * ph + BLK * i + n
                        J = STEPS * ph + i - 1
                        k = LN_STACK[ph] + i - 1
                        yb = batch_cols(Y, (i - 1) % B) if prev else None

                        def chunk(j):
                            bk, u = j % 2, 4 * G + j
                            dve.wait_ge(sq_done, u + 1)
                            vec.reduce_sum(SS[:, 8 * j:8 * j + 8],
                                           SQ[:, bk, :].rearrange("p (h f) -> p h f", f=LD), axis=AX)\
                               .then_inc(ss_done, 1)
                            dve.wait_ge(rot_add, seen(u - 1))
                            src = QBK[bk].rearrange("p (h f) -> p h f", f=LD)
                            tab = TAB[:, n, 2 * (j // 2), :].unsqueeze(1).broadcast_to([128, 8, LD])
                            vec.tensor_tensor(out=T1[:, bk, :].rearrange("p (h f) -> p h f", f=LD), in0=src,
                                              in1=tab, op=ALU.mult).then_inc(rot_mul, 1)
                            src = QBK[bk].rearrange("p (h z f) -> p h z f", z=2, f=LD // 2)
                            tab = TAB[:, n, 2 * (j // 2) + 1, :].rearrange("p (z f) -> p z f", z=2).unsqueeze(1)\
                                .broadcast_to([128, 8, 2, LD // 2])
                            dst = T2[:, bk, :].rearrange("p (h z f) -> p h z f", z=2, f=LD // 2)[:, :, ::-1, :]
                            vec.tensor_tensor(out=dst, in0=src, in1=tab, op=ALU.mult).then_inc(rot_mul, 1)

                        if cur:
                            dve.wait_ge(tab_ready, GX + 1)
                            chunk(0)
                            chunk(1)
                        if has_prev:
                            for sl in range(2):
                                dve.wait_ge(s_mm, 2 * G - 1 + sl)
                                sc = SB[sl][:, :].rearrange("p (h k) -> p h k", k=LD)
                                vec.tensor_reduce(out=MXS[:, sl, :], in_=sc, op=ALU.max, axis=AX)\
                                   .then_inc(max_done, 1)
                                dve.wait_ge(max_done, 2 * G - 1 + sl)
                                dve.wait_ge(d_mm, seen(2 * (G - 1)))
                                vec.tensor_tensor(out=PB[:, :, sl, :], in0=sc,
                                                  in1=MXS[:, sl, :].unsqueeze(2).broadcast_to([128, HP, LD]),
                                                  op=ALU.subtract).then_inc(sub_done, 1)
                        if cur:
                            chunk(2)
                            chunk(3)
                            dve.wait_ge(ss_done, 4 * G + 4)
                            rsqrt(SV[:, :], SY[:, :], SA[:, :], SS[:, :], ALU.max, 1e-24, rn_step, RN * G,
                                  qk_norm, seen(4 * G))
                        if has_prev:
                            for sl in range(2):
                                dve.wait_ge(exp_done, 2 * G - 1 + sl)
                                vec.reduce_sum(SMS[:, sl, :], PB[:, :, sl, :], axis=AX).then_inc(sum_done, 1)
                            dve.wait_ge(sum_done, 2 * G)
                            dve.wait_ge(on_ready, seen(2 * (G - 1)))
                            vec.reciprocal(RSS[:, :, :], SMS[:, :, :]).then_inc(rs_done, 1)
                        if prev and n == 1:
                            dve.wait_ge(wo_mm, J + 1)
                            vec.tensor_tensor(out=yb, in0=MB[0][:, :], in1=yb, op=ALU.add).then_inc(y_attn, 1)
                            dve.wait_ge(y_attn, J + 1)
                            vec.tensor_scalar(out=XF[0:64, :], in0=Y[0:64, bass.ds(((i - 1) % B) * T, T)],
                                              scalar1=1.0, scalar2=None, op0=ALU.mult)
                            vec.tensor_copy(XF[64:128, 1:T], Y[64:128, bass.ds(((i - 1) % B) * T, T - 1)])\
                               .then_inc(ln_in, 1)
                        if prev and n == 2:
                            ln_center(k)
                        if prev and n == 3:
                            for t in range(FT):
                                dve.wait_ge(gelu_done, FT * J + t + 1)
                                dve.wait_ge(a_mm, FT * J + t + 1)
                                r = FR[t]
                                vec.scalar_tensor_tensor(out=HT[0:r, t, :], in0=MB[1][0:r, :],
                                                         scalar=PAR[0:r, P_B1A + t:P_B1A + t + 1],
                                                         in1=GG[0:r, t, :], op0=ALU.add, op1=ALU.mult)\
                                   .then_inc(h_ready, 1)
                        if has_prev:
                            dve.wait_ge(rs_done, G)
                            for sl in range(2):
                                dve.wait_ge(e_mm, 2 * G - 1 + sl)
                                vec.tensor_tensor(out=ON[:, :, sl, :],
                                                  in0=TB[sl].rearrange("p (h d) -> p h d", d=LD),
                                                  in1=RSS[:, sl, :].unsqueeze(2).broadcast_to([128, HP, LD]),
                                                  op=ALU.mult).then_inc(on_ready, 1)
                        if cur:
                            if n == 0:
                                dve.wait_ge(v_mm, seen(4 * G))
                                prep(i, BLK - 1, GX + BLK)
                            else:
                                dve.wait_ge(v_mm, 4 * (G + 1))
                                dve.wait_ge(y_ready, (B + STEPS) * ph + i + 2)
                                prep(i + 1, n - 1, GX + BLK)
                        if prev and n == 2:
                            ln_scale(k, XN[:, :], xn_aff)
                            dve.wait_ge(xn_aff, B + STEPS * ph + i)
                            dve.wait_ge(par_ready, J + 1)
                            vec.tensor_scalar(out=XN[:, :], in0=XN[:, :], scalar1=PAR[:, P_G:P_G + 1],
                                              scalar2=PAR[:, P_B:P_B + 1], op0=ALU.mult, op1=ALU.add)\
                               .then_inc(xn_ready, 1)
                        if prev and n == 3:
                            dve.wait_ge(w2_mm, J + 1)
                            vec.scalar_tensor_tensor(out=yb, in0=MB[0][:, :], scalar=PAR[:, P_B2:P_B2 + 1], in1=yb,
                                                     op0=ALU.add, op1=ALU.add).then_inc(y_ready, 1)

                body(0, True, False)
                with dve.Fori(1, STEPS) as i:
                    body(i, True, True)
                body(STEPS, False, True)
                dve.wait_ge(y_ready, (B + STEPS) * (ph + 1))

            dve.wait_ge(x_ready, 4)
            dve.wait_ge(vecs_loaded, 16 * VEC_LOADS)
            part(0)
            stack(0)
            part(1)
            stack(1)
            vec.tensor_tensor(out=X[:, :], in0=X[:, :], in1=Y[:, :], op=ALU.add).then_inc(o_ready, 1)

        @block.tensor
        def _(pe):
            ten = nc.tensor
            pe.wait_ge(con_loaded, 16)
            pe.wait_ge(x_loaded, 16)
            for g in range(4):
                pe.wait_ge(x_ready, seen(g - 1))
                for m in range(4):
                    last = ten.transpose(TB[g % 2][:, 128 * m:128 * m + 128], XL[:, g, 128 * m:128 * m + 128], IDF)
                last.then_inc(x_t, 1)
            pe.wait_ge(mats_loaded, 16 * 6)
            for m in range(3):
                last = ten.transpose(SB[0][:, 128 * m:128 * m + 128], WB[:, m, :], IDF)
            last.then_inc(wb_t, 1)
            pe.wait_ge(consts, 3)

            def part(p):
                wm = WA if p == 0 else WB
                if p == 0:
                    pe.wait_ge(wb_ready, 1)
                    pe.wait_ge(x_ready, 4)
                else:
                    pe.wait_ge(y_ready, B + STEPS)

                def body(b):
                    c = B * p + b
                    for z in range(2 - p):
                        k = LN_PART[p] + (3 - p) * b + z
                        ln_mean_mm(k)
                        ln_var_mm(k)
                    pe.wait_ge(xn_part, c + 1)
                    ten.matmul(MB[0][:, :], wm[:, 0, :], XN[:, :], start=True, stop=True).then_inc(q_mm, 1)
                    ten.matmul(MB[1][:, :], wm[:, 1, :], XN[:, :], start=True, stop=True).then_inc(k_mm, 1)
                    pe.wait_ge(chain, (LINKS[0] * c + 1) if p == 0 else (LINKS[0] * B + LINKS[1] * b + 2))
                    for m in range(4):
                        last = ten.matmul(MB[0][:, 128 * m:128 * m + 128], XN[:, 128 * m:128 * m + 128], wm[:, 2, :],
                                          start=True, stop=True)
                    last.then_inc(vp_mm, 1)
                    pe.wait_ge(va_ready, c + 1)
                    if p == 0:
                        pe.wait_ge(qs_loaded, 16 * 12 * (c + 1))
                    else:
                        pe.wait_ge(qs_ordered, 2 * (b + 1))

                    def score_max(u):
                        if u >= 2:
                            pe.wait_ge(max_red, 64 * c + u - 1)
                        ten.matmul(MB[u % 2][:, :], QS[0:SROWS, u // 4, 128 * (u % 4):128 * (u % 4) + 128],
                                   KS[0:SROWS, u // 4, :], start=True, stop=True).then_inc(smax_mm, 1)

                    def maxima(hh):
                        pe.wait_ge(nm_ready, 2 * c + hh + 1)
                        ten.transpose(MB[0][0:32, 0:128], MX[:, :], IDF).then_inc(nm_t, 1)

                    def pv(un):
                        g, kb = un // 4, un % 4
                        pe.wait_ge(exp_p, 32 * c + 2 * un + 2)
                        if kb == 0 and g >= 2:
                            pe.wait_ge(os_ready, 4 * c + g - 1)
                        for j in range(4):
                            last = ten.matmul(OB[g % 2][32 * j:32 * j + 32, :], VA[:, 4 * g + j, kb, :],
                                              PX[:, un % 2, j, :], start=(kb == 0), stop=(kb == 3))
                        last.then_inc(pv_mm, 1)

                    def unit(un):
                        g, kb = un // 4, un % 4
                        for j in range(4):
                            if un >= 1 and j % 2 == 0:
                                pe.wait_ge(exp_p, 32 * c + 2 * (un - 1) + j // 2 + 1)
                            last = ten.matmul(R4[:, j, :], KS[0:SROWS + PARTS, 4 * g + j, 128 * kb:128 * kb + 128],
                                              QS[0:SROWS + PARTS, 4 * g + j, :], start=True, stop=True)
                            if j % 2 == 1:
                                last.then_inc(st_mm, 1)

                    for u in range(32):
                        score_max(u)
                    maxima(0)
                    pe.wait_ge(mt_ready, 2 * c + 1)
                    for un in range(8):
                        if un == 0:
                            for u in range(32, 36):
                                score_max(u)
                            pe.wait_ge(m_loaded, 32 * c + 16)
                        unit(un)
                        if un < 7:
                            for u in range(36 + 4 * un, 40 + 4 * un):
                                score_max(u)
                        if un >= 1:
                            pv(un - 1)
                    maxima(1)
                    pv(7)
                    pe.wait_ge(m_loaded, 32 * c + 32)
                    for un in range(8, 16):
                        unit(un)
                        if un >= 9:
                            pv(un - 1)
                    pv(15)
                    for g in range(4):
                        pe.wait_ge(os_ready, 4 * c + g + 1)
                        if g == 0:
                            pe.wait_ge(mt_ready, 2 * c + 2)
                        if g >= 2:
                            pe.wait_ge(on_part, 4 * c + g - 1)
                        ten.matmul(MB[g % 2][:, :], SELB, OS[:, g, :], start=True, stop=True).then_inc(den_mm, 1)
                    if p == 1:
                        for z in range(2):
                            pe.wait_ge(stat_in, 2 * b + z + 1)
                            ten.matmul(MB[0][:, 0:1], AVG[:, :], STAT[:, 1 + 3 * z:2 + 3 * z], start=True, stop=True)\
                               .then_inc(stat_mm, 1)
                    k = LN_PART[p] + (3 - p) * b + (2 - p)
                    ln_mean_mm(k)
                    ln_var_mm(k)
                part_loop(pe, body)

            def stack(ph):
                pe.wait_ge(y_ready, (B + STEPS) * ph + B)

                def body(i, cur, prev):
                    for n in range(BLK):
                        has_prev = (cur and n > 0) or (prev and n == 0)
                        G = BLK * STEPS * ph + BLK * i + n
                        GX = (BLK * STEPS + BLK - 1) * ph + BLK * i + n
                        J = STEPS * ph + i - 1
                        k = LN_STACK[ph] + i - 1
                        first_prev = isinstance(i, int) and i == 0 and n == 1
                        pn = (n - 1) % BLK
                        x0 = WIN + 128 * n

                        def proj(j):
                            u = 4 * G + j
                            pe.wait_ge(rot_mul, seen(2 * (u - 1)))
                            pe.wait_ge(sq_done, seen(u - 1))
                            ten.matmul(QBK[j % 2], XS[:, x0:x0 + 128], W[:, (i // B) % 2, T * j:T * j + T],
                                       start=True, stop=True).then_inc(qk_mm, 1)

                        if cur:
                            pe.wait_ge(xs_ready, GX + 1)
                            if n == 0:
                                pe.wait_ge(wqkv_loaded, 16 * (LAYERS * ph + i // B + 1))
                            proj(0)
                            proj(1)
                        if has_prev:
                            pe.wait_ge(qt_ready, 4 * G)
                            for sl in range(2):
                                pe.wait_ge(sub_done, seen(2 * (G - 2) + sl + 1))
                                ten.matmul(SB[sl][:, :], IDB[:, :], MASKB[:, 1 if pn == 0 else 0, :].unsqueeze(1)
                                           .broadcast_to([128, HP, 2 * WIN]), start=True, stop=True)
                                for hp in range(HP):
                                    for g in range(4):
                                        r = 64 * (sl ^ (g >= 2))
                                        last = ten.matmul(
                                            SB[sl][32 * g:32 * g + 32, 64 * hp:64 * hp + 64],
                                            QT[r:r + 64, hp, 32 * g:32 * g + 32],
                                            KT[r:r + 64, pn, hp, 32 * g:32 * g + 64],
                                            start=False, stop=True, skip_group_check=True)
                                last.then_inc(s_mm, 1)
                        if cur:
                            proj(2)
                            proj(3)
                            for v in range(4):
                                pe.wait_ge(v_ready, seen(4 * G + v - 1))
                                if v == 0 and n == 0 and prev:
                                    pe.wait_ge(y_ready, (B + STEPS) * ph + i + 3)
                                if v == 0 and n == 2 and prev:
                                    pe.wait_ge(y_attn, J + 1)
                                if v == 1 and n == 3 and prev:
                                    pe.wait_ge(ln_step, RN * k + 1)
                                wv = W[:, (i // B) % 2, 2 * INNER:3 * INNER]\
                                    .rearrange("p (h z f) -> p h z f", z=2, f=LD)[:, :, v // 2, :]
                                if v < 2:
                                    lo = x0 - WIN * v
                                    ten.matmul(MB[v % 2][:, :], XS[:, lo:lo + 128], wv, start=True, stop=True)\
                                       .then_inc(v_mm, 1)
                                else:
                                    ten.matmul(MB[v % 2][:, :], XSW[:, n, v - 2, :], wv, start=True, stop=True)\
                                       .then_inc(v_mm, 1)
                        if has_prev:
                            pe.wait_ge(exp_done, 2 * G)
                            for z in range(2):
                                if not first_prev:
                                    pe.wait_ge(ot_ready, 2 * G - 3 + z)
                                for hp in range(4 * z, 4 * z + 4):
                                    last = ten.transpose(TB[z][:, 128 * (hp % 4):128 * (hp % 4) + 128],
                                                         PB[:, hp, :, :].rearrange("p s k -> p (s k)"), IDF)
                                last.then_inc(d_mm, 1)
                        if prev and n == 1:
                            pe.wait_ge(ot_ready, 2 * BLK * (STEPS * ph + i))
                            pe.wait_ge(wo_loaded, 48 * (LAYERS * ph + (i - 1) // B + 1))
                            if cur:
                                pe.wait_ge(v_ready, 4 * G + 3)
                            else:
                                pe.wait_ge(y_ready, (B + STEPS) * ph + i + 3)
                            for half in range(2):
                                for hp in range(HP):
                                    view = OT[:, hp, :].rearrange("p (n z t) -> p n z t", n=BLK, z=2)[:, :, half, :]
                                    dst = MB[0][:, :].rearrange("p (n z t) -> p n z t", n=BLK, z=2)[:, :, half, :]
                                    last = ten.matmul(dst, WO[:, half, hp, :], view, start=(hp == 0),
                                                      stop=(hp == HP - 1))
                            last.then_inc(wo_mm, 1)
                        if prev and n == 2:
                            if cur:
                                pe.wait_ge(v_ready, 4 * G + 3)
                            ln_mean_mm(k)
                        if prev and n == 3:
                            pe.wait_ge(xn_ready, J + 1)
                            pe.wait_ge(w12_loaded, 48 * (LAYERS * ph + (i - 1) // B + 1))
                            for t in range(FT):
                                r = FR[t]
                                if t == 0 and cur:
                                    pe.wait_ge(v_ready, 4 * G + 3)
                                if t > 0:
                                    pe.wait_ge(gelu_done, FT * J + t)
                                ten.matmul(MB[0][0:r, :], W1[:, FF + 128 * t:FF + 128 * t + r], XN[:, :],
                                           start=True, stop=True).then_inc(gate_mm, 1)
                                if t == 0 and cur:
                                    pe.wait_ge(v_ready, 4 * G + 4)
                                if t > 0:
                                    pe.wait_ge(h_ready, FT * J + t)
                                ten.matmul(MB[1][0:r, :], W1[:, 128 * t:128 * t + r], XN[:, :],
                                           start=True, stop=True).then_inc(a_mm, 1)
                        if has_prev:
                            pe.wait_ge(pt_ready, 2 * G)
                            pe.wait_ge(v_ready, 4 * G).then_inc(pv_turn, 1)
                            for sl in range(2):
                                for hp in range(HP):
                                    for g in range(4):
                                        par = sl ^ (g >= 2)
                                        r = 64 * sl
                                        last = ten.matmul(
                                            TB[sl][32 * g:32 * g + 32, 64 * hp:64 * hp + 64],
                                            PT[r:r + 64, hp, 32 * g:32 * g + 32],
                                            VT[r:r + 64, pn % 2, 2 * par + (g + 1) % 2, 64 * hp:64 * hp + 64],
                                            start=True, stop=True)
                                last.then_inc(e_mm, 1)
                        if prev and n == 2:
                            if cur:
                                pe.wait_ge(v_ready, 4 * G + 4)
                            ln_var_mm(k)
                        if cur:
                            for j in range(4):
                                if j < 2 and has_prev:
                                    pe.wait_ge(on_ready, 2 * G - 1 + j)
                                if j >= 2:
                                    pe.wait_ge(qt_ready, 4 * G + j - 1)
                                pe.wait_ge(qk_norm, 4 * G + j + 1)
                                for m in range(4):
                                    last = ten.transpose(TB[j % 2][:, 128 * m:128 * m + 128],
                                                         QN[:, j, 128 * m:128 * m + 128], IDF)
                                last.then_inc(b_mm, 1)
                        if has_prev:
                            pe.wait_ge(on_ready, 2 * G)
                            for z in range(2):
                                if cur:
                                    pe.wait_ge(qt_ready, 4 * G + z + 3)
                                for hp in range(4 * z, 4 * z + 4):
                                    last = ten.transpose(TB[z][:, 128 * (hp % 4):128 * (hp % 4) + 128],
                                                         ON[:, hp, :, :].rearrange("p s k -> p (s k)"), IDF)
                                last.then_inc(g_mm, 1)
                        if prev and n == 3:
                            pe.wait_ge(h_ready, FT * (J + 1))
                            for t in range(FT):
                                r = FR[t]
                                last = ten.matmul(MB[0][:, :], W2[0:r, t, :], HT[0:r, t, :], start=(t == 0),
                                                  stop=(t == FT - 1))
                            last.then_inc(w2_mm, 1)

                body(0, True, False)
                with pe.Fori(1, STEPS) as i:
                    body(i, True, True)
                body(STEPS, False, True)

            part(0)
            stack(0)
            part(1)
            stack(1)
            pe.wait_ge(o_ready, 1)
            for g in range(4):
                pe.wait_ge(o_ready, seen(g))
                for m in range(4):
                    last = ten.transpose(TB[g % 2][:, 128 * m:128 * m + 128],
                                         X[:, T * g + 128 * m:T * g + 128 * m + 128], IDF)
                last.then_inc(o_t, 1)

        @block.scalar
        def _(act):
            sca = nc.scalar
            for g in range(4):
                act.wait_ge(x_t, g + 1)
                sca.activation(X[:, T * g:T * g + T], TB[g % 2], ACT.Copy).then_inc(x_ready, 1)
            act.wait_ge(wb_t, 1)
            sca.activation(WB[:, :, :].rearrange("p m j -> p (m j)"), SB[0][:, 0:384], ACT.Copy)\
               .then_inc(wb_ready, 1)

            def part(p):
                def body(b):
                    c = B * p + b
                    for z in range(2 - p):
                        ln_square(LN_PART[p] + (3 - p) * b + z)
                    for un in range(16):
                        for z in range(2):
                            act.wait_ge(st_mm, 32 * c + 2 * un + z + 1)
                            if un >= 2 and z == 0:
                                act.wait_ge(pv_mm, 16 * c + un - 1)
                            sca.activation(PX[:, un % 2, 2 * z:2 * z + 2, :], R4[:, 2 * z:2 * z + 2, :], ACT.Exp)\
                               .then_inc(exp_p, 1)
                    ln_square(LN_PART[p] + (3 - p) * b + (2 - p))
                part_loop(act, body)

            def stack(ph):
                def body(i, cur, prev):
                    for n in range(BLK):
                        has_prev = (cur and n > 0) or (prev and n == 0)
                        G = BLK * STEPS * ph + BLK * i + n
                        J = STEPS * ph + i - 1
                        k = LN_STACK[ph] + i - 1
                        pn = (n - 1) % BLK

                        def square(j):
                            u = 4 * G + j
                            act.wait_ge(qk_mm, u + 1)
                            act.wait_ge(ss_done, seen(u - 1))
                            sca.activation(SQ[:, j % 2, :], QBK[j % 2], ACT.Square).then_inc(sq_done, 1)

                        if cur:
                            square(0)
                            square(1)
                        if has_prev:
                            for sl in range(2):
                                act.wait_ge(sub_done, 2 * G - 1 + sl)
                                sca.activation(PB[:, :, sl, :], PB[:, :, sl, :], ACT.Exp).then_inc(exp_done, 1)
                        if cur:
                            square(2)
                            square(3)
                            for v in range(4):
                                act.wait_ge(v_mm, 4 * G + v + 1)
                                sca.activation(VT[:, n % 2, v, :], MB[v % 2][:, :], ACT.Copy)\
                                   .then_inc(v_ready, 1)
                        if has_prev:
                            for z in range(2):
                                act.wait_ge(d_mm, 2 * G - 1 + z)
                                sca.activation(PT[:, 4 * z:4 * z + 4, :], TB[z].rearrange("p (h t) -> p h t", h=4),
                                               ACT.Copy).then_inc(pt_ready, 1)
                        if prev and n == 2:
                            ln_square(k)
                        if prev and n == 3:
                            act.wait_ge(par_ready, J + 1)
                            for t in range(FT):
                                r = FR[t]
                                act.wait_ge(gate_mm, FT * J + t + 1)
                                sca.activation(GG[0:r, t, :], MB[0][0:r, :], ACT.Gelu,
                                               bias=PAR[0:r, P_B1G + t:P_B1G + t + 1]).then_inc(gelu_done, 1)
                        if cur:
                            for j in range(4):
                                act.wait_ge(b_mm, 4 * G + j + 1)
                                tt = TB[j % 2].rearrange("p (h t) -> p h t", h=4)
                                if j < 2:
                                    dst = QT[:, 4 * j:4 * j + 4, :]
                                else:
                                    hs = slice(4 * (j - 2), 4 * (j - 2) + 4)
                                    dst = KT[:, n, hs, WIN:WIN + 128]
                                    if n + 1 < BLK:
                                        sca.activation(KT[:, n + 1, hs, 0:WIN], tt[:, :, 128 - WIN:128], ACT.Copy)
                                sca.activation(dst, tt, ACT.Copy).then_inc(qt_ready, 1)
                        if has_prev:
                            for z in range(2):
                                act.wait_ge(g_mm, 2 * G - 1 + z)
                                sca.activation(OT[:, 4 * z:4 * z + 4, 128 * pn:128 * pn + 128],
                                               TB[z].rearrange("p (h t) -> p h t", h=4), ACT.Copy)\
                                   .then_inc(ot_ready, 1)

                body(0, True, False)
                with act.Fori(1, STEPS) as i:
                    body(i, True, True)
                body(STEPS, False, True)

            part(0)
            stack(0)
            part(1)
            stack(1)
            for g in range(4):
                act.wait_ge(o_t, g + 1)
                sca.activation(XL[:, g, :], TB[g % 2], ACT.Copy).then_inc(o_ready, 1)

        @block.gpsimd
        def _(pool):
            gp = nc.gpsimd

            def part_init(p):
                if p == 1:
                    pool.wait_ge(y_ready, B + STEPS)
                gp.memset(KS[:, :, :], 1.0).then_inc(va_clear, 1)
                gp.memset(VA[:, :, :, 0:DH], 0.0)
                gp.memset(VA[:, :, :, DH + 1:32], 0.0)
                gp.memset(VA[:, :, :, DH:DH + 1], 1.0).then_inc(va_clear, 1)

            def stack(ph):
                pool.wait_ge(y_ready, (B + STEPS) * ph + B)

                def table(m, layer):
                    gp.tensor_tensor(out=TAB[:, m, :, :].rearrange("p (q c) f -> p q c f", q=2),
                                     in0=ROT[:, m, :, :].rearrange("p (q c) f -> p q c f", q=2),
                                     in1=QSC[:, layer, :, :].unsqueeze(2).broadcast_to([128, 2, 2, LD]),
                                     op=ALU.mult).then_inc(tab_ready, 1)
                for m in range(BLK - 1):
                    table(m, 0)

                def body(i, cur, prev):
                    for n in range(BLK):
                        G = BLK * STEPS * ph + BLK * i + n
                        J = STEPS * ph + i - 1
                        if prev and n == 0:
                            pool.wait_ge(y_ready, (B + STEPS) * ph + i + 3)
                            gp.tensor_copy(PAR[:, :], PARL[:, (i - 1) // B, :]).then_inc(par_ready, 1)
                        if not cur:
                            continue
                        for j in range(4):
                            u = 4 * G + j
                            pool.wait_ge(rot_mul, 2 * (u + 1))
                            pool.wait_ge(b_mm, seen(u - 3))
                            gp.tensor_tensor(out=QN[:, j, :], in0=T1[:, j % 2, :], in1=T2[:, j % 2, :], op=ALU.add)\
                              .then_inc(rot_add, 1)
                            if j == 0:
                                if n == 0:
                                    table(BLK - 1, i // B)
                                else:
                                    table(n - 1, ((i + 1) // B) % LAYERS)
                        pool.wait_ge(rn_step, RN * (G + 1))
                        pool.wait_ge(rot_add, 4 * G + 4)
                        for j in range(4):
                            v = QN[:, j, :].rearrange("p (h f) -> p h f", f=LD)
                            gp.tensor_tensor(out=v, in0=v, in1=SY[:, 8 * j:8 * j + 8].unsqueeze(2)
                                             .broadcast_to([128, 8, LD]), op=ALU.mult).then_inc(qk_norm, 1)

                body(0, True, False)
                with pool.Fori(1, STEPS) as i:
                    body(i, True, True)
                body(STEPS, False, True)

            gp.memset(PARL[:, :, :], 0.0).then_inc(parl_clear, 1)
            part_init(0)
            pool.wait_ge(vecs_loaded, 16 * VEC_LOADS)
            pool.wait_ge(con_loaded, 16)
            stack(0)
            part_init(1)
            stack(1)

        @block.sync
        def _(sp):
            sp.dma_start(CON[:, :], a["consts"]).then_inc(con_loaded, 16)
            sp.dma_start(XL[:, :, :].rearrange("p g (m f) -> p (g m) f", f=D),
                         a["L0_attn_a_x"].rearrange("b t f -> (b t) f").rearrange("(n p) f -> p n f", p=128))\
              .then_inc(x_loaded, 16)
            for z, name in enumerate(("Wq", "Wk", "Wv")):
                sp.dma_start(WA[:, z, :], a["L0_attn_a_" + name]).then_inc(mats_loaded, 16)
                sp.dma_start(WB[:, z, :], a["L0_attn_b_" + name]).then_inc(mats_loaded, 16)

            def col(ap):
                return ap.rearrange("(p o) -> p o", o=1)

            def load_layer(L, layer):
                sp.dma_start(W[:, L % 2, :], a["L0_ffn_Wqkv"][layer, :, :]).then_inc(wqkv_loaded, 16)

            def load_wo(layer):
                wo = a["L0_ffn_Wo"][layer, :, :].rearrange("(h p) m -> p h m", p=128)
                sp.dma_start(WO[:, 0, :, :], wo).then_inc(wo_loaded, 16)
                sp.dma_start(WO[0:64, 1, :, :], wo[64:128]).then_inc(wo_loaded, 16)
                sp.dma_start(WO[64:128, 1, :, :], wo[0:64]).then_inc(wo_loaded, 16)

            def load_w12(layer):
                w2 = a["L0_ffn_W2"][layer, :, :]
                full = 128 * (FT - 1)
                sp.dma_start(W1[:, :], a["L0_ffn_W1"][layer, :, :]).then_inc(w12_loaded, 16)
                sp.dma_start(W2[:, 0:FT - 1, :], w2[0:full, :].rearrange("(t p) m -> p t m", p=128))\
                  .then_inc(w12_loaded, 16)
                sp.dma_start(W2[0:FR[-1], FT - 1, :], w2[full:FF, :]).then_inc(w12_loaded, 16)

            with nc.allow_non_contiguous_dma(reason="vectors by partition, once"):
                for z, name in enumerate(("bq", "bk", "ln_g", "ln_b")):
                    sp.dma_start(VEC[:, z:z + 1], col(a["L0_attn_a_" + name])).then_inc(vecs_loaded, 16)
                sp.dma_start(BVB[:, :], a["L0_attn_a_bv"].rearrange("(o f) -> o f", o=1).broadcast_to([128, 128]))\
                  .then_inc(vecs_loaded, 16)
                sp.wait_ge(parl_clear, 1)
                for t in range(FT):
                    r = FR[t]
                    for c0, o in ((P_B1A, 0), (P_B1G, FF)):
                        sp.dma_start(PARL[0:r, :, c0 + t],
                                     a["L0_ffn_b1"][:, o + 128 * t:o + 128 * t + r].rearrange("l p -> p l"))\
                          .then_inc(vecs_loaded, 16)
                for c0, name in ((P_B2, "b2"), (P_G, "ln_g"), (P_B, "ln_b")):
                    sp.dma_start(PARL[:, :, c0], a["L0_ffn_" + name].rearrange("l p -> p l"))\
                      .then_inc(vecs_loaded, 16)
                for z, name in enumerate(("q_scale", "k_scale")):
                    src = a["L0_ffn_" + name].rearrange("(o l) f -> o l f", o=1).broadcast_to([128, LAYERS, LD])
                    sp.dma_start(QSC[:, :, z, :], src).then_inc(vecs_loaded, 16)
            load_layer(0, 0)
            load_layer(1, 1)
            load_wo(0)
            load_w12(0)

            def part(p):
                def body(b):
                    c = B * p + b
                    sp.wait_ge(parts_ready, 2 * c + 2)
                    sp.dma_start(scr_parts.rearrange("k p t -> p k t"), PTS[:, :, :]).then_inc(scr_written, 16)
                    sp.wait_ge(scr_written, 16 * (c + 1))
                    sp.wait_ge(va_clear, 2 * p + 1)
                    for r in range(len(Q_PARTS)):
                        for z, (dst, src) in enumerate(((QS, Q_PARTS), (KS, K_PARTS))):
                            rows = dst[DH * r:DH * r + DH, :, :] if p == 0 else \
                                STG[64 * z + DH * r:64 * z + DH * r + DH, :, :]
                            sp.dma_start(rows,
                                         scr_parts[PARTS * z + src[r], :, :].rearrange("(h d) t -> d h t", d=DH))\
                              .then_inc(qs_loaded, 16)
                    for hh in range(2):
                        sp.wait_ge(mt_ready, 2 * c + hh + 1)
                        sp.dma_start(scr_max[:, 32 * hh:32 * hh + 32, :].rearrange("k u q -> u k q"), MT[:, :, :])\
                          .then_inc(m_written, 16)
                        sp.wait_ge(m_written, 16 * (2 * c + hh + 1))
                        half = scr_max[:, 32 * hh:32 * hh + 32, :]
                        sp.dma_start(QS[SROWS:SROWS + PARTS, 8 * hh:8 * hh + 8, :],
                                     half.rearrange("k (h q) t -> k h (q t)", h=8)).then_inc(m_loaded, 16)
                    sp.wait_ge(on_part, 4 * c + 4)
                    if p == 0:
                        for j in range(4):
                            sp.dma_start(scr_att.rearrange("(g j d) t -> j d g t", j=4, d=DH)[j],
                                         OS[32 * j:32 * j + DH, :, :]).then_inc(att_written, 16)
                        written = 64 * (c + 1)
                    else:
                        for j in range(4):
                            for g in range(4):
                                dst = scr_att.rearrange("(c d) (g j t) -> g j d c t", d=DH, g=4, j=4)[g, j]
                                sp.dma_start(dst, OS[32 * j:32 * j + DH, g, :].rearrange("d (c t) -> d c t", t=32))\
                                  .then_inc(att_written, 16)
                        written = 64 * B + 256 * (b + 1)
                    sp.wait_ge(att_written, written)
                    sp.dma_start(ATT, scr_att).then_inc(att_loaded, 16)
                part_loop(sp, body)

            def stack(ph):
                def body(layer):
                    L = LAYERS * ph + layer
                    sp.wait_ge(v_mm, 4 * BLK * B * (L + 1))
                    load_layer(layer, (layer + 2) % LAYERS)
                    sp.wait_ge(wo_mm, B * (L + 1))
                    load_wo((layer + 1) % LAYERS)
                    sp.wait_ge(y_ready, (B + STEPS) * ph + B * (layer + 2))
                    load_w12((layer + 1) % LAYERS)
                if ph == 0:
                    with sp.Fori(0, LAYERS) as layer:
                        body(layer)
                else:
                    with sp.Fori(0, LAYERS - 2) as layer:
                        body(layer)
                    sp.wait_ge(wo_mm, B * (2 * LAYERS - 1))
                    load_wo(LAYERS - 1)
                    sp.wait_ge(y_ready, (B + STEPS) + B * LAYERS)
                    load_w12(LAYERS - 1)

            part(0)
            stack(0)
            part(1)
            stack(1)
            for g in range(4):
                sp.wait_ge(o_ready, g + 2)
                sp.dma_start(out[g, :, :].rearrange("(m p) f -> p m f", p=128),
                             XL[:, g, :].rearrange("p (m f) -> p m f", f=D)).then_inc(o_stored, 16)
            sp.wait_ge(o_stored, 64)


_INS = ['L0_attn_a_x', 'L0_attn_a_ln_g', 'L0_attn_a_ln_b', 'L0_attn_a_Wq', 'L0_attn_a_bq', 'L0_attn_a_Wk',
        'L0_attn_a_bk', 'L0_attn_a_Wv', 'L0_attn_a_bv', 'L0_attn_b_Wq', 'L0_attn_b_Wk', 'L0_attn_b_Wv',
        'L0_ffn_Wqkv', 'L0_ffn_q_scale', 'L0_ffn_k_scale', 'L0_ffn_Wo', 'L0_ffn_ln_g', 'L0_ffn_ln_b',
        'L0_ffn_W1', 'L0_ffn_b1', 'L0_ffn_W2', 'L0_ffn_b2']


def kernel(**inputs):
    import numpy as _np
    import concourse.bacc as _bacc
    from concourse import mybir as _mybir
    from concourse.bass_utils import run_bass_kernel_spmd as _run

    nc = _bacc.Bacc("TRN2", target_bir_lowering=False, num_devices=1)
    arrays = {f"in_{n}_dram": _np.ascontiguousarray(inputs[n]) for n in _INS}
    arrays["in_consts_dram"] = host_constants()
    aps = {n: nc.dram_tensor(f"in_{n}_dram", arrays[f"in_{n}_dram"].shape,
                             _mybir.dt.from_np(arrays[f"in_{n}_dram"].dtype), kind="ExternalInput").ap()
           for n in [*_INS, "consts"]}
    out = nc.dram_tensor("out_0_dram", (B, T, D), F32, kind="ExternalOutput").ap()
    scr_parts = nc.dram_tensor("scr_parts", (2 * PARTS, 128, T), BF16).ap()
    scr_max = nc.dram_tensor("scr_max", (PARTS, 64, 128), BF16).ap()
    scr_att = nc.dram_tensor("scr_att", (128, T), F32).ap()
    hybrid_kernel(nc, aps, out, scr_parts, scr_max, scr_att)
    r = _run(nc, [arrays], core_ids=[0])
    return r.results[0]["out_0_dram"]
```

```python
import numpy as np

import concourse.bass as bass
from concourse import mybir
from contextlib import ExitStack

F32 = mybir.dt.float32
BF16 = mybir.dt.bfloat16
I32 = mybir.dt.int32
ALU = mybir.AluOpType
ACT = mybir.ActivationFunctionType
AX = mybir.AxisListType.X

B, T, D = 4, 512, 128
N = B * T
EPS = 1e-5
NH, DH = 16, 8
QB4 = T // 128
PARTS = 3
Q_PARTS = (0, 0, 1, 1, 0, 2)
K_PARTS = (0, 1, 0, 1, 2, 0)
SROWS = DH * len(Q_PARTS)
MROW = 96
LAYERS = 6
LH, LD = 16, 64
INNER = LH * LD
WIN = 32
FF = int(D * 4 * 2 / 3)
FT = (FF + 127) // 128
FR = [min(128, FF - 128 * t) for t in range(FT)]
HP = LH // 2
STEPS = LAYERS * B
BLK = T // 128
QK_SCALE = 8.0
MASKED = -1e37
MAGIC = 1597463007.0
NEWTON = 3
RN = 3 + 3 * NEWTON
P_B1A, P_B1G, P_B2, P_G, P_B, NPAR = 0, FT, 2 * FT, 2 * FT + 1, 2 * FT + 2, 2 * FT + 3
LN_PART = [0, 3 * B + STEPS]
LN_STACK = [3 * B, 3 * B + STEPS + 2 * B]
V_COPIES = ((0, 32, 0, 96, False), (0, 0, 96, 32, True), (2, 0, 96, 32, False), (2, 32, 0, 32, False),
            (2, 96, 64, 32, False), (2, 64, 32, 32, True))
SHIFTS = len(V_COPIES)
VEC_LOADS = 5 + 2 * FT + 3 + 2
LINKS = [31, 50]


def host_constants():
    half = np.arange(0, LD, 2, dtype=np.float32)
    inv_freq = (np.float32(1.0) / np.float32(10000.0) ** (half / np.float32(LD))).astype(np.float32)
    t = np.arange(T, dtype=np.float32)
    freqs = (t[:, None] * inv_freq[None, :]).astype(np.float32)
    freqs = np.concatenate([freqs, freqs], -1)
    base = ((half + np.float32(0.4 * LD)) / np.float32(1.4 * LD)).astype(np.float32)
    power = ((t - T // 2) / (WIN // 2)).astype(np.float32)
    scale = (base[None, :] ** power[:, None]).astype(np.float32)
    scale = np.concatenate([scale, scale], -1)
    cos, sin = np.cos(freqs), np.sin(freqs)
    sign = np.where(np.arange(LD) < LD // 2, 1.0, -1.0).astype(np.float32)
    inv = (np.float32(1.0) / scale).astype(np.float32)
    kinds = [cos * scale, np.roll(sin * scale, LD // 2, 1) * sign, cos * inv, np.roll(sin * inv, LD // 2, 1) * sign]
    kinds[0], kinds[1] = kinds[0] * np.float32(QK_SCALE), kinds[1] * np.float32(QK_SCALE)
    rot = np.stack(kinds, 1).reshape(BLK, 128, 4, LD).transpose(1, 0, 2, 3).reshape(128, -1)
    r = np.arange(128)[:, None] % WIN
    k = np.arange(2 * WIN)[None, :]
    bad = (r > k) | (k > r + WIN)
    mask = np.stack([bad, bad | ((k < WIN) & (np.arange(128)[:, None] < WIN))], 1).reshape(128, -1) * MASKED
    return np.concatenate([rot, mask, np.eye(128)], 1).astype(np.float32)


C_ROT, C_MASK = 0, BLK * 4 * LD
C_ID = C_MASK + 2 * 2 * WIN
NCON = C_ID + 128


def hybrid_kernel(nc, a, out, scr_parts, scr_max, scr_att):
    with ExitStack() as ctx:
        def sb(name, shape, dt=F32):
            return ctx.enter_context(nc.sbuf_tensor(name, shape, dt))

        def sem(name):
            return ctx.enter_context(nc.semaphore(name))

        X = sb("X", [128, N])
        Y = sb("Y", [128, N])
        CON = sb("CON", [128, NCON])
        IDB = sb("IDB", [128, 128], BF16)
        MASKB = sb("MASKB", [128, 2, 2 * WIN], BF16)
        AVG = sb("AVG", [128, 128])
        IDF = CON[:, C_ID:C_ID + 128]
        ROT = CON[:, C_ROT:C_MASK].rearrange("p (n k f) -> p n k f", n=BLK, k=4)
        XF = sb("XF", [128, T])
        XC = sb("XC", [128, T])
        XQ = sb("XQ", [128, T])
        XN = sb("XN", [128, T])
        NV = sb("NV", [128, T // 128])
        NY = sb("NY", [128, T // 128])
        NA = sb("NA", [128, T // 128])
        WA = sb("WA", [128, 3, 128])
        WB = sb("WB", [128, 3, 128])
        VEC = sb("VEC", [128, 4])
        BVB = sb("BVB", [128, 128])
        W = sb("W", [128, 2, 3 * INNER])
        WO = sb("WO", [128, 2, HP, D])
        W1 = sb("W1", [128, 2 * FF])
        W2 = sb("W2", [128, FT, D])
        PARL = sb("PARL", [128, LAYERS, NPAR])
        PARN = sb("PARN", [128, NPAR])
        PARF = sb("PARF", [128, NPAR])
        QSC = sb("QSC", [128, LAYERS, 2, LD])
        TAB = sb("TAB", [128, BLK, 4, LD])
        XS = sb("XS", [128, T])
        XSW = sb("XSW", [128, BLK, 128])
        ROTB = sb("ROTB", [128, 6 * T])
        SQ = ROTB[:, 0:2 * T].rearrange("p (r t) -> p r t", r=2)
        T1 = ROTB[:, 2 * T:4 * T].rearrange("p (r t) -> p r t", r=2)
        T2 = ROTB[:, 4 * T:6 * T].rearrange("p (r t) -> p r t", r=2)
        SS = sb("SS", [128, 32])
        SV = sb("SV", [128, 32])
        SY = sb("SY", [128, 32])
        SA = sb("SA", [128, 32])
        QN = sb("QN", [128, 4, T])
        QT = sb("QT", [128, HP, 128])
        KT = sb("KT", [128, BLK, HP, WIN + 128])
        VT = sb("VT", [128, 2, 4, T])
        PB = sb("PB", [128, HP, 2, LD])
        PT = sb("PT", [128, HP, 128])
        ON = sb("ON", [128, HP, 2, LD])
        OT = sb("OT", [128, HP, T])
        MXS = sb("MXS", [128, 2, HP])
        SMS = sb("SMS", [128, 2, HP])
        RSS = sb("RSS", [128, 2, HP])
        GG = sb("GG", [128, FT, T])
        HT = sb("HT", [128, FT, T])
        QS = KT[:, :, :, :].rearrange("p n h t -> p (n h t)")[:, 0:NH * T // 2].bitcast(BF16)\
            .rearrange("p (h t) -> p h t", h=NH)
        KS = OT[:, :, :].rearrange("p h t -> p (h t)").bitcast(BF16).rearrange("p (h t) -> p h t", h=NH)
        STG = VT[:, :, :, :].rearrange("p r v t -> p (r v t)").bitcast(BF16).rearrange("p (c t) -> p c t", c=NH)
        PX = VT
        VA = ROTB[:, 0:4 * T].rearrange("p (h k d) -> p h k d", h=NH, k=QB4)
        PTS = GG[:, :, :].rearrange("p a t -> p (a t)").bitcast(BF16).rearrange("p (a t) -> p a t", t=T)
        QF, KF, RES = HT[:, 0, :], HT[:, 1, :], HT[:, 2, :]
        OS = QN
        ATT = PT[:, 4:8, :]
        MX = SS[:, 0:16]
        RD = PB[:, 0, 0, :]
        AQ = PT[:, 0:4, :]
        MXA = sb("MXA", [128, 64])
        MT = sb("MT", [16, PARTS, 128], BF16)
        MR = sb("MR", [16, 128])
        STAT = sb("STAT", [128, 8])
        XL = QN

        def bank(name):
            return ctx.enter_context(nc.psum_tensor(name, [128, T], F32))

        R4 = ctx.enter_context(nc.psum_tensor("R4", [128, 4, T], F32))
        QBK = [R4[:, 0, :], R4[:, 1, :]]
        TB = [R4[:, 2, :], R4[:, 3, :]]
        SB = [bank("S0"), bank("S1")]
        MB = [bank("M0"), bank("M1")]
        OB = SB
        QKB = [SB[0][:, :], SB[1][:, :], TB[0], TB[1]]

        con_loaded = sem("con_loaded")
        mats_loaded = sem("mats_loaded")
        vecs_loaded = sem("vecs_loaded")
        consts = sem("consts")
        parl_clear = sem("parl_clear")
        x_loaded = sem("x_loaded")
        x_t = sem("x_t")
        x_ready = sem("x_ready")
        wb_t = sem("wb_t")
        wb_ready = sem("wb_ready")
        ln_in = sem("ln_in")
        ln_mean = sem("ln_mean")
        ln_xc = sem("ln_xc")
        ln_sq = sem("ln_sq")
        ln_var = sem("ln_var")
        ln_spread = sem("ln_spread")
        ln_step = sem("ln_step")
        zeros = sem("zeros")
        y_ready = sem("y_ready")
        xn_aff = sem("xn_aff")
        xn_part = sem("xn_part")
        q_mm = sem("q_mm")
        k_mm = sem("k_mm")
        vp_mm = sem("vp_mm")
        chain = sem("chain")
        va_clear = sem("va_clear")
        va_ready = sem("va_ready")
        parts_ready = sem("parts_ready")
        scr_written = sem("scr_written")
        qs_loaded = sem("qs_loaded")
        qs_ordered = sem("qs_ordered")
        smax_mm = sem("smax_mm")
        max_red = sem("max_red")
        nm_ready = sem("nm_ready")
        nm_t = sem("nm_t")
        mt_ready = sem("mt_ready")
        m_written = sem("m_written")
        m_loaded = sem("m_loaded")
        st_mm = sem("st_mm")
        exp_p = sem("exp_p")
        pv_mm = sem("pv_mm")
        os_ready = sem("os_ready")
        os_t = sem("os_t")
        att_t = sem("att_t")
        att_out = sem("att_out")
        on_part = sem("on_part")
        att_written = sem("att_written")
        att_loaded = sem("att_loaded")
        stat_in = sem("stat_in")
        stat_mm = sem("stat_mm")
        wqkv_loaded = sem("wqkv_loaded")
        wo_loaded = sem("wo_loaded")
        w1_loaded = sem("w1_loaded")
        w2_loaded = sem("w2_loaded")
        xs_copied = sem("xs_copied")
        xs_ready = sem("xs_ready")
        tab_ready = sem("tab_ready")
        parn_ready = sem("parn_ready")
        parf_ready = sem("parf_ready")
        qk_mm = sem("qk_mm")
        sq_done = sem("sq_done")
        ss_done = sem("ss_done")
        rot_mul = sem("rot_mul")
        rot_add = sem("rot_add")
        rn_step = sem("rn_step")
        q_norm = sem("q_norm")
        k_norm = sem("k_norm")
        b_mm = sem("b_mm")
        qt_ready = sem("qt_ready")
        s_mm = sem("s_mm")
        pv_turn = sem("pv_turn")
        max_done = sem("max_done")
        sub_done = sem("sub_done")
        exp_done = sem("exp_done")
        sum_done = sem("sum_done")
        rs_done = sem("rs_done")
        v_mm = sem("v_mm")
        v_ready = sem("v_ready")
        v_shifted = sem("v_shifted")
        d_mm = sem("d_mm")
        pt_ready = sem("pt_ready")
        e_mm = sem("e_mm")
        on_ready = sem("on_ready")
        g_mm = sem("g_mm")
        ot_ready = sem("ot_ready")
        wo_mm = sem("wo_mm")
        y_attn = sem("y_attn")
        xn_ready = sem("xn_ready")
        gate_mm = sem("gate_mm")
        gelu_done = sem("gelu_done")
        a_mm = sem("a_mm")
        h_ready = sem("h_ready")
        w2_mm = sem("w2_mm")
        o_t = sem("o_t")
        o_ready = sem("o_ready")
        o_stored = sem("o_stored")

        def seen(count):
            return max(count, 0) if isinstance(count, int) else count

        block = ctx.enter_context(nc.Block())

        def batch_cols(t, b):
            return t[:, bass.ds(b * T, T)]

        def rsqrt(v, y, tmp, src, op, const, step, base, y_users=None, y_used=0):
            vec = nc.vector
            vec.tensor_scalar(out=v, in0=src, scalar1=const, scalar2=None, op0=op).then_inc(step, 1)
            vec.wait_ge(step, base + 1)
            vec.tensor_scalar(out=tmp.bitcast(I32), in0=v.bitcast(I32), scalar1=1, scalar2=None,
                              op0=ALU.logical_shift_right).then_inc(step, 1)
            vec.wait_ge(step, base + 2)
            if y_users is not None:
                vec.wait_ge(y_users, y_used)
            vec.tensor_scalar(out=y.bitcast(I32), in0=tmp.bitcast(I32), scalar1=-1.0, scalar2=MAGIC,
                              op0=ALU.mult, op1=ALU.add).then_inc(step, 1)
            for it in range(NEWTON):
                vec.wait_ge(step, base + 3 + 3 * it)
                vec.tensor_tensor(out=tmp, in0=v, in1=y, op=ALU.mult).then_inc(step, 1)
                vec.wait_ge(step, base + 4 + 3 * it)
                vec.scalar_tensor_tensor(out=tmp, in0=tmp, scalar=-0.5, in1=y, op0=ALU.mult, op1=ALU.mult)\
                   .then_inc(step, 1)
                vec.wait_ge(step, base + 5 + 3 * it)
                vec.scalar_tensor_tensor(out=y, in0=tmp, scalar=1.5, in1=y, op0=ALU.add, op1=ALU.mult)\
                   .then_inc(step, 1)
            vec.wait_ge(step, base + RN)

        def ln_center(k):
            nc.vector.wait_ge(ln_mean, k + 1)
            nc.vector.tensor_tensor(out=XC[:, :], in0=XF[:, :], in1=MB[0][:, :], op=ALU.subtract)\
                .then_inc(ln_xc, 1)

        def ln_root(k):
            nc.vector.wait_ge(ln_var, k + 1)
            rsqrt(NV[:, :], NY[:, :], NA[:, :], MB[1][:, 0:T // 128], ALU.add, EPS, ln_step, RN * k)

        def ln_apply(k, dst, signal):
            nc.vector.wait_ge(ln_spread, k + 1)
            nc.vector.tensor_tensor(out=dst, in0=XC[:, :], in1=MB[1][:, :], op=ALU.mult).then_inc(signal, 1)

        def ln_scale(k, dst, signal):
            ln_root(k)
            ln_apply(k, dst, signal)

        def ln_mean_mm(k):
            nc.tensor.wait_ge(ln_in, k + 1)
            nc.tensor.matmul(MB[0][:, :], AVG[:, :], XF[:, :], start=True, stop=True).then_inc(ln_mean, 1)

        def ln_var_mm(k):
            nc.tensor.wait_ge(ln_sq, k + 1)
            for m in range(T // 128):
                last = nc.tensor.matmul(MB[1][:, m:m + 1], XQ[:, 128 * m:128 * m + 128], AVG[:, 0:1],
                                        start=True, stop=True)
            last.then_inc(ln_var, 1)

        def ln_spread_mm(k):
            nc.tensor.wait_ge(ln_step, RN * (k + 1))
            for m in range(T // 128):
                last = nc.tensor.matmul(MB[1][:, 128 * m:128 * m + 128], NY[:, m:m + 1].broadcast_to([128, 128]),
                                        IDF, start=True, stop=True)
            last.then_inc(ln_spread, 1)

        def ln_square(k):
            nc.scalar.wait_ge(ln_xc, k + 1)
            nc.scalar.activation(XQ[:, :], XC[:, :], ACT.Square).then_inc(ln_sq, 1)

        def part_loop(eng, body):
            body(0)
            with eng.Fori(1, B) as b:
                body(b)

        def own_norm(p, b):
            return LN_PART[p] + (3 - p) * b - (0 if isinstance(b, int) and b == 0 else 1)

        def stack_norm(p, b):
            return LN_PART[p] + (3 - p) * b + (1 - p if not (isinstance(b, int) and b == B) else -1)

        @block.vector
        def _(dve):
            vec = nc.vector
            dve.wait_ge(con_loaded, 16)
            vec.tensor_copy(IDB[:, :], IDF).then_inc(consts, 1)
            vec.tensor_copy(MASKB[:, :, :], CON[:, C_MASK:C_ID].rearrange("p (m k) -> p m k", m=2))\
               .then_inc(consts, 1)
            vec.memset(AVG[:, :], 1.0 / D).then_inc(consts, 1)

            def part(p):
                def body(b):
                    c = B * p + b
                    count = [0]
                    base = LINKS[0] * c if p == 0 else LINKS[0] * B + LINKS[1] * b

                    def link(ins):
                        count[0] += 1
                        ins.then_inc(chain, 1)
                        dve.wait_ge(chain, base + count[0])

                    xb = batch_cols(X, b)
                    k0 = own_norm(p, b)
                    if p == 0:
                        vec.tensor_scalar(out=XF[:, :], in0=xb, scalar1=1.0, scalar2=None, op0=ALU.mult)\
                            .then_inc(ln_in, 1)
                        ln_center(k0)
                        ln_scale(k0, XF[:, :], ln_in)
                        dve.wait_ge(ln_in, k0 + 2)
                        k0 = k0 + 1
                        ln_center(k0)
                        ln_scale(k0, XN[:, :], xn_aff)
                        dve.wait_ge(xn_aff, b + 1)
                        vec.tensor_scalar(out=XN[:, :], in0=XN[:, :], scalar1=VEC[:, 2:3], scalar2=VEC[:, 3:4],
                                          op0=ALU.mult, op1=ALU.add).then_inc(xn_part, 1)
                    else:
                        link(vec.tensor_tensor(out=xb, in0=xb, in1=batch_cols(Y, b), op=ALU.add))
                        vec.tensor_scalar(out=XF[:, :], in0=xb, scalar1=1.0, scalar2=None, op0=ALU.mult)\
                            .then_inc(ln_in, 1)
                        ln_center(k0)
                        ln_scale(k0, XN[:, :], xn_part)
                    dve.wait_ge(q_mm, c + 1)
                    if p == 0:
                        link(vec.tensor_scalar(out=QF, in0=MB[0][:, :], scalar1=VEC[:, 0:1],
                                               scalar2=float(1.0 / np.sqrt(DH)), op0=ALU.add, op1=ALU.mult))
                    else:
                        link(vec.tensor_copy(QF, MB[0][:, :]))
                    dve.wait_ge(k_mm, c + 1)
                    if p == 0:
                        link(vec.tensor_scalar(out=KF, in0=MB[1][:, :], scalar1=VEC[:, 1:2], scalar2=None,
                                               op0=ALU.add))
                    else:
                        link(vec.tensor_copy(KF, MB[1][:, :]))
                    dve.wait_ge(vp_mm, c + 1)
                    dve.wait_ge(va_clear, 2 * p + 2)
                    if p == 0:
                        vec.tensor_tensor(
                            out=VA[:, :, :, 0:DH].rearrange("p h k d -> p k h d"),
                            in0=MB[0][:, :].rearrange("p (k h d) -> p k h d", k=QB4, h=NH),
                            in1=BVB[:, :].rearrange("p (h d) -> p h d", h=NH).unsqueeze(1)
                            .broadcast_to([128, QB4, NH, DH]), op=ALU.add).then_inc(va_ready, 1)
                    else:
                        for j in range(4):
                            for cc in range(4):
                                src = MB[0][32 * j:32 * j + 32, :].rearrange(
                                    "t (n k c d) -> t n k c d", n=4, k=4, c=4)[:, :, :, cc, :]
                                last = vec.tensor_copy(VA[32 * cc:32 * cc + 32, j::4, :, 0:DH], src)
                        last.then_inc(va_ready, 1)
                    for z, f in enumerate((QF, KF)):
                        first = vec.tensor_copy(PTS[:, PARTS * z, :], f)
                        link(first)
                        link(vec.tensor_tensor(out=RES, in0=f, in1=PTS[:, PARTS * z, :], op=ALU.subtract))
                        link(vec.tensor_copy(PTS[:, PARTS * z + 1, :], RES))
                        link(vec.tensor_tensor(out=RES, in0=RES, in1=PTS[:, PARTS * z + 1, :], op=ALU.subtract))
                        vec.tensor_copy(PTS[:, PARTS * z + 2, :], RES).then_inc(parts_ready, 1)
                        dve.wait_ge(parts_ready, 2 * c + z + 1)

                    if not (isinstance(b, int) and b == 0):
                        stack_input(b)
                    if p == 1:
                        dve.wait_ge(qs_loaded, 16 * 12 * (c + 1))
                        dve.wait_ge(va_clear, 2 * p + 1)
                        for z, dst in enumerate((QS, KS)):
                            vec.tensor_copy(dst[0:SROWS, :, :].rearrange("r h (c t) -> r h c t", t=32),
                                            STG[64 * z:64 * z + SROWS, :, :].rearrange("r c (h t) -> r h c t", t=32))\
                               .then_inc(qs_ordered, 1)

                    def sums(g):
                        dve.wait_ge(pv_mm, 16 * c + 4 * g + 4)
                        vec.tensor_copy(OS[:, g, :], OB[g % 2][:, :]).then_inc(os_ready, 1)

                    for g in range(4):
                        for u in range(16 * g, 16 * g + 16):
                            dve.wait_ge(smax_mm, 64 * c + u + 1)
                            vec.tensor_reduce(out=MXA[:, u:u + 1], in_=MB[u % 2][:, :], op=ALU.max, axis=AX)\
                               .then_inc(max_red, 1)
                            if u % 16 == 7 and g >= 2:
                                sums(g - 2)
                        dve.wait_ge(max_red, 64 * c + 16 * g + 16)
                        vec.tensor_scalar(out=MX, in0=MXA[:, 16 * g:16 * g + 16], scalar1=-1.0, scalar2=None,
                                          op0=ALU.mult).then_inc(nm_ready, 1)
                        dve.wait_ge(nm_t, 4 * c + g + 1)
                        if g >= 1:
                            dve.wait_ge(m_written, 16 * (4 * c + g))
                        mps = MB[0][0:16, 0:128]
                        link(vec.tensor_copy(MT[:, 0, :], mps))
                        link(vec.tensor_tensor(out=MR[:, :], in0=mps, in1=MT[:, 0, :], op=ALU.subtract))
                        link(vec.tensor_copy(MT[:, 1, :], MR[:, :]))
                        link(vec.tensor_tensor(out=MR[:, :], in0=MR[:, :], in1=MT[:, 1, :], op=ALU.subtract))
                        vec.tensor_copy(MT[:, 2, :], MR[:, :]).then_inc(mt_ready, 1)
                        dve.wait_ge(mt_ready, 4 * c + g + 1)
                    sums(2)
                    sums(3)
                    for g in range(4):
                        dve.wait_ge(os_t, 4 * c + g + 1)
                        by_query = R4[:, g, :].rearrange("p (m j e) -> p m j e", m=4, j=4)
                        rd = RD[:, 16 * g:16 * g + 16].rearrange("p (m j) -> p m j", m=4)
                        link(vec.reciprocal(rd, by_query[:, :, :, DH]))
                        vec.tensor_tensor(out=AQ[:, :, 32 * g:32 * g + 32].rearrange("p m (j d) -> p m j d", j=4),
                                          in0=by_query[:, :, :, 0:DH],
                                          in1=rd.unsqueeze(3).broadcast_to([128, 4, 4, DH]), op=ALU.mult)\
                           .then_inc(on_part, 1)
                    dve.wait_ge(att_t, c + 1)
                    if p == 0:
                        link(vec.tensor_tensor(out=xb, in0=xb, in1=MB[0][:, :], op=ALU.add))
                    else:
                        vec.tensor_copy(OS[:, 0, :], MB[0][:, :]).then_inc(att_out, 1)
                        dve.wait_ge(att_loaded, 16 * (T // 32) * (b + 1))
                        link(vec.tensor_tensor(out=XC[:, :], in0=ATT.rearrange("p m t -> p (m t)"),
                                               in1=XN[:, :], op=ALU.add))
                        link(vec.reduce_sum(STAT[:, 0:1], XC[:, :], axis=AX))
                        vec.tensor_scalar(out=STAT[:, 1:2], in0=STAT[:, 0:1], scalar1=1.0 / T, scalar2=None,
                                          op0=ALU.mult).then_inc(stat_in, 1)
                        dve.wait_ge(stat_mm, 2 * b + 1)
                        link(vec.tensor_copy(STAT[:, 2:3], MB[0][:, 0:1]))
                        link(vec.tensor_scalar(out=XC[:, :], in0=XC[:, :], scalar1=STAT[:, 2:3], scalar2=None,
                                               op0=ALU.subtract))
                        link(vec.tensor_tensor(out=XF[:, :], in0=XC[:, :], in1=XC[:, :], op=ALU.mult))
                        link(vec.reduce_sum(STAT[:, 3:4], XF[:, :], axis=AX))
                        vec.tensor_scalar(out=STAT[:, 4:5], in0=STAT[:, 3:4], scalar1=1.0 / T, scalar2=None,
                                          op0=ALU.mult).then_inc(stat_in, 1)
                        dve.wait_ge(stat_mm, 2 * b + 2)
                        rsqrt(STAT[:, 5:6], STAT[:, 6:7], STAT[:, 7:8], MB[0][:, 0:1], ALU.add, EPS, chain,
                              base + count[0])
                        count[0] += RN
                        link(vec.scalar_tensor_tensor(out=xb, in0=XC[:, :], scalar=STAT[:, 6:7], in1=xb,
                                                      op0=ALU.mult, op1=ALU.add))
                    assert count[0] == LINKS[p], (p, count[0])

                def stack_input(b):
                    kl = stack_norm(p, b)
                    vec.tensor_scalar(out=XF[:, :], in0=batch_cols(X, b - 1), scalar1=1.0, scalar2=None,
                                      op0=ALU.mult).then_inc(ln_in, 1)
                    ln_center(kl)
                    ln_scale(kl, batch_cols(Y, b - 1), y_ready)
                    dve.wait_ge(y_ready, (B + STEPS) * p + b)

                part_loop(dve, body)
                stack_input(B)

            def stack(ph):
                def prep(i, m, done):
                    b = (i % B) * T
                    lo = 1 if m == 0 else 0
                    vec.tensor_scalar(out=XS[0:64, 128 * m:128 * m + 128],
                                      in0=Y[0:64, bass.ds(b + 128 * m, 128)], scalar1=1.0, scalar2=None,
                                      op0=ALU.mult)
                    vec.tensor_copy(XS[64:128, 128 * m + lo:128 * m + 128],
                                    Y[64:128, bass.ds(b + 128 * m + lo - 1, 128 - lo)]).then_inc(xs_copied, 1)
                    dve.wait_ge(xs_copied, done)
                    vec.tensor_copy(XSW[:, m, :].rearrange("p (z t) -> p z t", z=2),
                                    XS[:, 128 * m:128 * m + 128].rearrange("p (z t) -> p z t", z=2)[:, ::-1, :])\
                       .then_inc(xs_ready, 1)

                vec.memset(XS[64:128, 0:1], 0.0).then_inc(zeros, 1)
                vec.memset(KT[:, 0, :, 0:WIN], 0.0).then_inc(zeros, 1)
                vec.memset(XF[64:128, 0:1], 0.0).then_inc(zeros, 1)
                dve.wait_ge(zeros, 3 * ph + 3)
                for m in range(BLK - 1):
                    prep(0, m, (BLK * STEPS + BLK - 1) * ph + m + 1)

                def body(i, cur, prev, prev2):
                    for n in range(BLK):
                        has_prev = (cur and n > 0) or (prev and n == 0)
                        G = BLK * STEPS * ph + BLK * i + n
                        GX = (BLK * STEPS + BLK - 1) * ph + BLK * i + n
                        J = STEPS * ph + i - 1
                        J2 = J - 1
                        k = LN_STACK[ph] + i - 1

                        def gated(t, step, par):
                            dve.wait_ge(gelu_done, FT * step + t + 1)
                            dve.wait_ge(a_mm, FT * step + t + 1)
                            r = FR[t]
                            vec.scalar_tensor_tensor(out=HT[0:r, t, :], in0=MB[1][0:r, :],
                                                     scalar=par[0:r, P_B1A + t:P_B1A + t + 1],
                                                     in1=GG[0:r, t, :], op0=ALU.add, op1=ALU.mult)\
                               .then_inc(h_ready, 1)

                        def chunk(j):
                            bk, u = j % 2, 4 * G + j
                            dve.wait_ge(sq_done, u + 1)
                            vec.reduce_sum(SS[:, 8 * j:8 * j + 8],
                                           SQ[:, bk, :].rearrange("p (h f) -> p h f", f=LD), axis=AX)\
                               .then_inc(ss_done, 1)
                            dve.wait_ge(rot_add, seen(u - 1))
                            src = QBK[bk].rearrange("p (h f) -> p h f", f=LD)
                            tab = TAB[:, n, 2 * (j // 2), :].unsqueeze(1).broadcast_to([128, 8, LD])
                            vec.tensor_tensor(out=T1[:, bk, :].rearrange("p (h f) -> p h f", f=LD), in0=src,
                                              in1=tab, op=ALU.mult).then_inc(rot_mul, 1)
                            src = QBK[bk].rearrange("p (h z f) -> p h z f", z=2, f=LD // 2)
                            tab = TAB[:, n, 2 * (j // 2) + 1, :].rearrange("p (z f) -> p z f", z=2).unsqueeze(1)\
                                .broadcast_to([128, 8, 2, LD // 2])
                            dst = T2[:, bk, :].rearrange("p (h z f) -> p h z f", z=2, f=LD // 2)[:, :, ::-1, :]
                            vec.tensor_tensor(out=dst, in0=src, in1=tab, op=ALU.mult).then_inc(rot_mul, 1)

                        if cur:
                            dve.wait_ge(tab_ready, GX + 1)
                            chunk(0)
                            chunk(1)
                        if prev and n == 2:
                            ln_center(k)
                        if prev and n == 3:
                            ln_apply(k, XN[:, :], xn_aff)
                            dve.wait_ge(xn_aff, B + STEPS * ph + i)
                            dve.wait_ge(parn_ready, J + 1)
                            vec.tensor_scalar(out=XN[:, :], in0=XN[:, :], scalar1=PARN[:, P_G:P_G + 1],
                                              scalar2=PARN[:, P_B:P_B + 1], op0=ALU.mult, op1=ALU.add)\
                               .then_inc(xn_ready, 1)
                        if has_prev:
                            for sl in range(2):
                                dve.wait_ge(s_mm, 2 * G - 1 + sl)
                                sc = SB[sl][:, :].rearrange("p (h k) -> p h k", k=LD)
                                vec.tensor_reduce(out=MXS[:, sl, :], in_=sc, op=ALU.max, axis=AX)\
                                   .then_inc(max_done, 1)
                                dve.wait_ge(max_done, 2 * G - 1 + sl)
                                dve.wait_ge(d_mm, seen(2 * (G - 1)))
                                vec.tensor_tensor(out=PB[:, :, sl, :], in0=sc,
                                                  in1=MXS[:, sl, :].unsqueeze(2).broadcast_to([128, HP, LD]),
                                                  op=ALU.subtract).then_inc(sub_done, 1)
                        if cur:
                            chunk(2)
                            chunk(3)
                            dve.wait_ge(ss_done, 4 * G + 4)
                            rsqrt(SV[:, :], SY[:, :], SA[:, :], SS[:, :], ALU.max, 1e-24, rn_step, RN * G,
                                  k_norm, seen(2 * G))
                            dve.wait_ge(rot_add, 4 * G + 2)
                            for j in range(2):
                                v = QN[:, j, :].rearrange("p (h f) -> p h f", f=LD)
                                vec.tensor_tensor(out=v, in0=v, in1=SY[:, 8 * j:8 * j + 8].unsqueeze(2)
                                                  .broadcast_to([128, 8, LD]), op=ALU.mult).then_inc(q_norm, 1)
                        if has_prev:
                            for sl in range(2):
                                dve.wait_ge(exp_done, 2 * G - 1 + sl)
                                vec.reduce_sum(SMS[:, sl, :], PB[:, :, sl, :], axis=AX).then_inc(sum_done, 1)
                            dve.wait_ge(sum_done, 2 * G)
                            dve.wait_ge(on_ready, seen(2 * (G - 1)))
                            vec.reciprocal(RSS[:, :, :], SMS[:, :, :]).then_inc(rs_done, 1)
                        if prev and n == 1:
                            yb = batch_cols(Y, (i - 1) % B)
                            dve.wait_ge(wo_mm, J + 1)
                            vec.tensor_tensor(out=yb, in0=MB[0][:, :], in1=yb, op=ALU.add).then_inc(y_attn, 1)
                            dve.wait_ge(y_attn, J + 1)
                            vec.tensor_scalar(out=XF[0:64, :], in0=Y[0:64, bass.ds(((i - 1) % B) * T, T)],
                                              scalar1=1.0, scalar2=None, op0=ALU.mult)
                            vec.tensor_copy(XF[64:128, 1:T], Y[64:128, bass.ds(((i - 1) % B) * T, T - 1)])\
                               .then_inc(ln_in, 1)
                        if prev2 and n == 0:
                            dve.wait_ge(parf_ready, J2 + 1)
                            gated(1, J2, PARF)
                        if has_prev:
                            dve.wait_ge(rs_done, G)
                            for sl in range(2):
                                dve.wait_ge(e_mm, 2 * G - 1 + sl)
                                vec.tensor_tensor(out=ON[:, :, sl, :],
                                                  in0=TB[sl].rearrange("p (h d) -> p h d", d=LD),
                                                  in1=RSS[:, sl, :].unsqueeze(2).broadcast_to([128, HP, LD]),
                                                  op=ALU.mult).then_inc(on_ready, 1)
                        if prev2 and n == 0:
                            gated(2, J2, PARF)
                        if prev and n == 2:
                            ln_root(k)
                        if prev and n == 3:
                            gated(0, J, PARN)
                        if cur:
                            if n == 0:
                                dve.wait_ge(v_mm, seen(2 * G))
                                prep(i, BLK - 1, GX + BLK)
                            else:
                                dve.wait_ge(v_mm, 2 * G)
                                dve.wait_ge(y_ready, (B + STEPS) * ph + i + 2)
                                prep(i + 1, n - 1, GX + BLK)
                        if prev2 and n == 2:
                            yb = batch_cols(Y, (i - 2) % B)
                            dve.wait_ge(w2_mm, J2 + 1)
                            vec.scalar_tensor_tensor(out=yb, in0=MB[0][:, :], scalar=PARF[:, P_B2:P_B2 + 1], in1=yb,
                                                     op0=ALU.add, op1=ALU.add).then_inc(y_ready, 1)

                body(0, True, False, False)
                body(1, True, True, False)
                with dve.Fori(2, STEPS) as i:
                    body(i, True, True, True)
                body(STEPS, False, True, True)
                body(STEPS + 1, False, False, True)
                dve.wait_ge(y_ready, (B + STEPS) * (ph + 1))

            dve.wait_ge(x_ready, 4)
            dve.wait_ge(vecs_loaded, 16 * VEC_LOADS)
            part(0)
            stack(0)
            part(1)
            stack(1)
            vec.tensor_tensor(out=X[:, :], in0=X[:, :], in1=Y[:, :], op=ALU.add).then_inc(o_ready, 1)

        @block.tensor
        def _(pe):
            ten = nc.tensor
            pe.wait_ge(con_loaded, 16)
            pe.wait_ge(x_loaded, 16)
            for g in range(4):
                pe.wait_ge(x_ready, seen(g - 1))
                for m in range(4):
                    last = ten.transpose(TB[g % 2][:, 128 * m:128 * m + 128], XL[:, g, 128 * m:128 * m + 128], IDF)
                last.then_inc(x_t, 1)
            pe.wait_ge(mats_loaded, 16 * 6)
            for m in range(3):
                last = ten.transpose(SB[0][:, 128 * m:128 * m + 128], WB[:, m, :], IDF)
            last.then_inc(wb_t, 1)
            pe.wait_ge(consts, 3)

            def part(p):
                wm = WA if p == 0 else WB
                if p == 0:
                    pe.wait_ge(wb_ready, 1)
                    pe.wait_ge(x_ready, 4)
                else:
                    pe.wait_ge(y_ready, B + STEPS)

                def body(b):
                    c = B * p + b
                    for z in range(2 - p):
                        k = own_norm(p, b) + z
                        ln_mean_mm(k)
                        ln_var_mm(k)
                        ln_spread_mm(k)
                    pe.wait_ge(xn_part, c + 1)
                    ten.matmul(MB[0][:, :], wm[:, 0, :], XN[:, :], start=True, stop=True).then_inc(q_mm, 1)
                    ten.matmul(MB[1][:, :], wm[:, 1, :], XN[:, :], start=True, stop=True).then_inc(k_mm, 1)
                    pe.wait_ge(chain, (LINKS[0] * c + 1) if p == 0 else (LINKS[0] * B + LINKS[1] * b + 2))
                    for m in range(4):
                        last = ten.matmul(MB[0][:, 128 * m:128 * m + 128], XN[:, 128 * m:128 * m + 128], wm[:, 2, :],
                                          start=True, stop=True)
                    last.then_inc(vp_mm, 1)
                    pe.wait_ge(va_ready, c + 1)
                    if not (isinstance(b, int) and b == 0):
                        stack_input(b)
                        pe.wait_ge(y_ready, (B + STEPS) * p + b)
                    if p == 0:
                        pe.wait_ge(qs_loaded, 16 * 12 * (c + 1))
                    else:
                        pe.wait_ge(qs_ordered, 2 * (b + 1))

                    def score_max(u):
                        if u >= 2:
                            pe.wait_ge(max_red, 64 * c + u - 1)
                        ten.matmul(MB[u % 2][:, :], QS[0:MROW, u // 4, 128 * (u % 4):128 * (u % 4) + 128],
                                   KS[0:MROW, u // 4, :], start=True, stop=True).then_inc(smax_mm, 1)

                    def maxima(g):
                        pe.wait_ge(nm_ready, 4 * c + g + 1)
                        ten.transpose(MB[0][0:16, 0:128], MX, IDF).then_inc(nm_t, 1)

                    def pv(un):
                        g, kb = un // 4, un % 4
                        pe.wait_ge(exp_p, 32 * c + 2 * un + 2)
                        if kb == 0 and g >= 2:
                            pe.wait_ge(os_ready, 4 * c + g - 1)
                        for j in range(4):
                            last = ten.matmul(OB[g % 2][32 * j:32 * j + 32, :], VA[:, 4 * g + j, kb, :],
                                              PX[:, un % 2, j, :], start=(kb == 0), stop=(kb == 3))
                        last.then_inc(pv_mm, 1)

                    def unit(un):
                        g, kb = un // 4, un % 4
                        for j in range(4):
                            if un >= 1 and j % 2 == 0:
                                pe.wait_ge(exp_p, 32 * c + 2 * (un - 1) + j // 2 + 1)
                            last = ten.matmul(R4[:, j, :], KS[:, 4 * g + j, 128 * kb:128 * kb + 128],
                                              QS[:, 4 * g + j, :], start=True, stop=True)
                            if j % 2 == 1:
                                last.then_inc(st_mm, 1)

                    for u in range(16):
                        score_max(u)
                    for g in range(4):
                        maxima(g)
                        pe.wait_ge(mt_ready, 4 * c + g + 1)
                        for u in range(16 * g + 16, 16 * g + 24):
                            if u < 64:
                                score_max(u)
                            if u % 8 == 3 and g >= 1:
                                pv(4 * g - 1)
                        pe.wait_ge(m_loaded, 16 * (4 * c + g + 1))
                        for k in range(4):
                            unit(4 * g + k)
                            for u in range(16 * g + 24 + 2 * k, 16 * g + 26 + 2 * k):
                                if u < 64:
                                    score_max(u)
                            if k >= 1:
                                pv(4 * g + k - 1)
                    pv(15)
                    for g in range(4):
                        pe.wait_ge(os_ready, 4 * c + g + 1)
                        if g == 0:
                            pe.wait_ge(exp_p, 32 * (c + 1))
                        for m in range(4):
                            last = ten.transpose(R4[:, g, 128 * m:128 * m + 128],
                                                 OS[:, g, 128 * m:128 * m + 128], IDF)
                        last.then_inc(os_t, 1)
                    pe.wait_ge(on_part, 4 * c + 4)
                    for m in range(4):
                        last = ten.transpose(MB[0][:, 128 * m:128 * m + 128], AQ[:, m, :], IDF)
                    last.then_inc(att_t, 1)
                    if p == 1:
                        for z in range(2):
                            pe.wait_ge(stat_in, 2 * b + z + 1)
                            ten.matmul(MB[0][:, 0:1], AVG[:, :], STAT[:, 1 + 3 * z:2 + 3 * z], start=True, stop=True)\
                               .then_inc(stat_mm, 1)

                def stack_input(b):
                    k = stack_norm(p, b)
                    ln_mean_mm(k)
                    ln_var_mm(k)
                    ln_spread_mm(k)

                part_loop(pe, body)
                stack_input(B)

            def stack(ph):
                pe.wait_ge(y_ready, (B + STEPS) * ph + B)

                def body(i, cur, prev, prev2):
                    for n in range(BLK):
                        has_prev = (cur and n > 0) or (prev and n == 0)
                        G = BLK * STEPS * ph + BLK * i + n
                        GX = (BLK * STEPS + BLK - 1) * ph + BLK * i + n
                        J = STEPS * ph + i - 1
                        J2 = J - 1
                        k = LN_STACK[ph] + i - 1
                        first_prev = isinstance(i, int) and i == 0 and n == 1
                        last_step = isinstance(i, int) and i == STEPS - 1
                        pn = (n - 1) % BLK
                        x0 = 128 * n

                        def proj(blk, step, m, j):
                            u = 4 * blk + j
                            pe.wait_ge(rot_mul, seen(2 * (u - 1)))
                            pe.wait_ge(sq_done, seen(u - 1))
                            ten.matmul(QBK[j % 2], XS[:, 128 * m:128 * m + 128],
                                       W[:, (step // B) % 2, T * j:T * j + T],
                                       start=True, stop=True).then_inc(qk_mm, 1)

                        if cur and isinstance(i, int) and i == 0 and n == 0:
                            pe.wait_ge(xs_ready, GX + 1)
                            pe.wait_ge(wqkv_loaded, 16 * (LAYERS * ph + 1))
                            proj(G, i, n, 0)
                            proj(G, i, n, 1)
                        def gate(t, step):
                            r = FR[t]
                            if t > 0:
                                pe.wait_ge(gelu_done, FT * step + t)
                            if cur:
                                pe.wait_ge(v_ready, 2 * G + 1)
                            elif t == 0:
                                pe.wait_ge(y_ready, (B + STEPS) * ph + i + 3)
                            ten.matmul(MB[0][0:r, :], W1[:, FF + 128 * t:FF + 128 * t + r], XN[:, :],
                                       start=True, stop=True).then_inc(gate_mm, 1)

                        def hidden(t, step):
                            r = FR[t]
                            if cur:
                                pe.wait_ge(v_ready, 2 * G + 2)
                            if t > 0:
                                pe.wait_ge(h_ready, FT * step + t)
                            ten.matmul(MB[1][0:r, :], W1[:, 128 * t:128 * t + r], XN[:, :],
                                       start=True, stop=True).then_inc(a_mm, 1)

                        if prev and n == 2:
                            ln_mean_mm(k)
                        if prev and n == 3:
                            ln_spread_mm(k)
                        if has_prev:
                            pe.wait_ge(qt_ready, 4 * G)
                            for sl in range(2):
                                if not first_prev:
                                    pe.wait_ge(ot_ready, 2 * G - 3 + sl)
                                ten.matmul(SB[sl][:, :], IDB[:, :], MASKB[:, 1 if pn == 0 else 0, :].unsqueeze(1)
                                           .broadcast_to([128, HP, 2 * WIN]), start=True, stop=True)
                                for hp in range(HP):
                                    for g in range(4):
                                        r = 64 * (sl ^ (g >= 2))
                                        last = ten.matmul(
                                            SB[sl][32 * g:32 * g + 32, 64 * hp:64 * hp + 64],
                                            QT[r:r + 64, hp, 32 * g:32 * g + 32],
                                            KT[r:r + 64, pn, hp, 32 * g:32 * g + 64],
                                            start=False, stop=True, skip_group_check=True)
                                last.then_inc(s_mm, 1)
                        if cur:
                            proj(G, i, n, 2)
                            proj(G, i, n, 3)
                            for v in range(2):
                                pe.wait_ge(v_ready, seen(2 * G + v - 1))
                                if n < 2 and prev2:
                                    pe.wait_ge(gelu_done if v == 0 else h_ready, FT * J2 + (1 if n == 0 else FT))
                                if v == 0 and n == 2 and prev:
                                    pe.wait_ge(ln_xc, k + 1)
                                if v == 0 and n == 3 and prev2:
                                    pe.wait_ge(y_ready, (B + STEPS) * ph + i + 3)
                                if v == 1 and n == 3 and prev:
                                    pe.wait_ge(xn_aff, B + STEPS * ph + i)
                                wv = W[:, (i // B) % 2, 2 * INNER:3 * INNER]\
                                    .rearrange("p (h z f) -> p h z f", z=2, f=LD)[:, :, v, :]
                                ten.matmul(MB[v][:, :], XS[:, x0:x0 + 128] if v == 0 else XSW[:, n, :], wv,
                                           start=True, stop=True).then_inc(v_mm, 1)
                        if has_prev:
                            pe.wait_ge(exp_done, 2 * G)
                            for z in range(2):
                                for hp in range(4 * z, 4 * z + 4):
                                    last = ten.transpose(TB[z][:, 128 * (hp % 4):128 * (hp % 4) + 128],
                                                         PB[:, hp, :, :].rearrange("p s k -> p (s k)"), IDF)
                                last.then_inc(d_mm, 1)
                        if prev and n == 1:
                            pe.wait_ge(ot_ready, 2 * BLK * (STEPS * ph + i))
                            pe.wait_ge(wo_loaded, 48 * (LAYERS * ph + (i - 1) // B + 1))
                            if cur:
                                pe.wait_ge(v_ready, 2 * G + 1)
                            elif prev2:
                                pe.wait_ge(gelu_done, FT * (J2 + 1))
                            for half in range(2):
                                for hp in range(HP):
                                    view = OT[:, hp, :].rearrange("p (n z t) -> p n z t", n=BLK, z=2)[:, :, half, :]
                                    dst = MB[0][:, :].rearrange("p (n z t) -> p n z t", n=BLK, z=2)[:, :, half, :]
                                    last = ten.matmul(dst, WO[:, half, hp, :], view, start=(hp == 0),
                                                      stop=(hp == HP - 1))
                            last.then_inc(wo_mm, 1)
                        if prev and n == 2:
                            if cur:
                                pe.wait_ge(v_ready, 2 * G + 2)
                            ln_var_mm(k)
                        if prev2 and n == 0:
                            gate(1, J2)
                            hidden(1, J2)
                        if prev2 and n == 2:
                            if cur:
                                pe.wait_ge(v_ready, 2 * G + 1)
                            elif prev:
                                pe.wait_ge(ln_xc, k + 1)
                            pe.wait_ge(h_ready, FT * (J2 + 1))
                            pe.wait_ge(w2_loaded, 32 * (LAYERS * ph + (i - 2) // B + 1))
                            for t in range(FT):
                                r = FR[t]
                                last = ten.matmul(MB[0][:, :], W2[0:r, t, :], HT[0:r, t, :], start=(t == 0),
                                                  stop=(t == FT - 1))
                            last.then_inc(w2_mm, 1)
                        if prev and n == 3:
                            pe.wait_ge(xn_ready, J + 1)
                            pe.wait_ge(w1_loaded, 16 * (LAYERS * ph + (i - 1) // B + 1))
                            gate(0, J)
                            hidden(0, J)
                        if has_prev:
                            pe.wait_ge(pt_ready, 2 * G)
                            pe.wait_ge(v_shifted, 16 * SHIFTS * G).then_inc(pv_turn, 1)
                            for sl in range(2):
                                for hp in range(HP):
                                    for g in range(4):
                                        par = sl ^ (g >= 2)
                                        r = 64 * sl
                                        last = ten.matmul(
                                            TB[sl][32 * g:32 * g + 32, 64 * hp:64 * hp + 64],
                                            PT[r:r + 64, hp, 32 * g:32 * g + 32],
                                            VT[r:r + 64, pn % 2, 2 * par + (g + 1) % 2, 64 * hp:64 * hp + 64],
                                            start=True, stop=True)
                                last.then_inc(e_mm, 1)
                        if prev2 and n == 0:
                            gate(2, J2)
                        if cur and not (last_step and n == BLK - 1):
                            step = i + (n + 1) // BLK
                            pe.wait_ge(xs_ready, GX + 2)
                            if n == BLK - 1:
                                pe.wait_ge(wqkv_loaded, 16 * (LAYERS * ph + step // B + 1))
                            proj(G + 1, step, (n + 1) % BLK, 0)
                            proj(G + 1, step, (n + 1) % BLK, 1)
                        if prev2 and n == 0:
                            hidden(2, J2)
                        if cur:
                            for j in range(4):
                                if j == 0 and has_prev:
                                    pe.wait_ge(sub_done, 2 * G)
                                if j >= 2 and has_prev:
                                    pe.wait_ge(on_ready, 2 * G - 3 + j)
                                if j < 2:
                                    pe.wait_ge(q_norm, 2 * G + j + 1)
                                else:
                                    pe.wait_ge(k_norm, 2 * G + j - 1)
                                for m in range(4):
                                    last = ten.transpose(QKB[j][:, 128 * m:128 * m + 128],
                                                         QN[:, j, 128 * m:128 * m + 128], IDF)
                                last.then_inc(b_mm, 1)
                        if has_prev:
                            pe.wait_ge(on_ready, 2 * G)
                            for z in range(2):
                                if cur:
                                    pe.wait_ge(qt_ready, 4 * G + z + 1)
                                for hp in range(4 * z, 4 * z + 4):
                                    last = ten.transpose(SB[z][:, 128 * (hp % 4):128 * (hp % 4) + 128],
                                                         ON[:, hp, :, :].rearrange("p s k -> p (s k)"), IDF)
                                last.then_inc(g_mm, 1)
                body(0, True, False, False)
                body(1, True, True, False)
                with pe.Fori(2, STEPS - 1) as i:
                    body(i, True, True, True)
                body(STEPS - 1, True, True, True)
                body(STEPS, False, True, True)
                body(STEPS + 1, False, False, True)

            part(0)
            stack(0)
            part(1)
            stack(1)
            pe.wait_ge(o_ready, 1)
            for g in range(4):
                pe.wait_ge(o_ready, seen(g))
                for m in range(4):
                    last = ten.transpose(TB[g % 2][:, 128 * m:128 * m + 128],
                                         X[:, T * g + 128 * m:T * g + 128 * m + 128], IDF)
                last.then_inc(o_t, 1)

        @block.scalar
        def _(act):
            sca = nc.scalar
            for g in range(4):
                act.wait_ge(x_t, g + 1)
                sca.activation(X[:, T * g:T * g + T], TB[g % 2], ACT.Copy).then_inc(x_ready, 1)
            act.wait_ge(wb_t, 1)
            sca.activation(WB[:, :, :].rearrange("p m j -> p (m j)"), SB[0][:, 0:384], ACT.Copy)\
               .then_inc(wb_ready, 1)

            def part(p):
                def body(b):
                    c = B * p + b
                    for z in range(2 - p):
                        ln_square(own_norm(p, b) + z)
                    if not (isinstance(b, int) and b == 0):
                        ln_square(stack_norm(p, b))
                    for un in range(16):
                        for z in range(2):
                            act.wait_ge(st_mm, 32 * c + 2 * un + z + 1)
                            if un >= 2 and z == 0:
                                act.wait_ge(pv_mm, 16 * c + un - 1)
                            sca.activation(PX[:, un % 2, 2 * z:2 * z + 2, :], R4[:, 2 * z:2 * z + 2, :], ACT.Exp)\
                               .then_inc(exp_p, 1)
                part_loop(act, body)
                ln_square(stack_norm(p, B))

            def stack(ph):
                def body(i, cur, prev, prev2):
                    for n in range(BLK):
                        has_prev = (cur and n > 0) or (prev and n == 0)
                        G = BLK * STEPS * ph + BLK * i + n
                        J = STEPS * ph + i - 1
                        J2 = J - 1
                        k = LN_STACK[ph] + i - 1
                        pn = (n - 1) % BLK

                        last_step = isinstance(i, int) and i == STEPS - 1

                        def gelu(t, step, par):
                            act.wait_ge(gate_mm, FT * step + t + 1)
                            sca.activation(GG[0:FR[t], t, :], MB[0][0:FR[t], :], ACT.Gelu,
                                           bias=par[0:FR[t], P_B1G + t:P_B1G + t + 1]).then_inc(gelu_done, 1)

                        def square(blk, j):
                            u = 4 * blk + j
                            act.wait_ge(qk_mm, u + 1)
                            act.wait_ge(ss_done, seen(u - 1))
                            sca.activation(SQ[:, j % 2, :], QBK[j % 2], ACT.Square).then_inc(sq_done, 1)

                        if cur and isinstance(i, int) and i == 0 and n == 0:
                            square(G, 0)
                            square(G, 1)
                        if prev and n == 2:
                            ln_square(k)
                        if has_prev:
                            for sl in range(2):
                                act.wait_ge(sub_done, 2 * G - 1 + sl)
                                sca.activation(PB[:, :, sl, :], PB[:, :, sl, :], ACT.Exp).then_inc(exp_done, 1)
                        if cur:
                            square(G, 2)
                            square(G, 3)
                            act.wait_ge(v_shifted, seen(16 * SHIFTS * G))
                            for v in range(2):
                                act.wait_ge(v_mm, 2 * G + v + 1)
                                sca.activation(VT[:, n % 2, 2 * v, :], MB[v][:, :], ACT.Copy)\
                                   .then_inc(v_ready, 1)
                        if has_prev:
                            for z in range(2):
                                act.wait_ge(d_mm, 2 * G - 1 + z)
                                sca.activation(PT[:, 4 * z:4 * z + 4, :], TB[z].rearrange("p (h t) -> p h t", h=4),
                                               ACT.Copy).then_inc(pt_ready, 1)
                        if prev2 and n == 0:
                            act.wait_ge(parf_ready, J2 + 1)
                            gelu(1, J2, PARF)
                            gelu(2, J2, PARF)
                        if prev and n == 3:
                            act.wait_ge(parn_ready, J + 1)
                            gelu(0, J, PARN)
                        if cur and not (last_step and n == BLK - 1):
                            square(G + 1, 0)
                            square(G + 1, 1)
                        if cur:
                            for j in range(4):
                                act.wait_ge(b_mm, 4 * G + j + 1)
                                tt = QKB[j].rearrange("p (h t) -> p h t", h=4)
                                if j < 2:
                                    dst = QT[:, 4 * j:4 * j + 4, :]
                                else:
                                    hs = slice(4 * (j - 2), 4 * (j - 2) + 4)
                                    dst = KT[:, n, hs, WIN:WIN + 128]
                                    if n + 1 < BLK:
                                        sca.activation(KT[:, n + 1, hs, 0:WIN], tt[:, :, 128 - WIN:128], ACT.Copy)
                                sca.activation(dst, tt, ACT.Copy).then_inc(qt_ready, 1)
                        if has_prev:
                            for z in range(2):
                                act.wait_ge(g_mm, 2 * G - 1 + z)
                                sca.activation(OT[:, 4 * z:4 * z + 4, 128 * pn:128 * pn + 128],
                                               SB[z][:, :].rearrange("p (h t) -> p h t", h=4), ACT.Copy)\
                                   .then_inc(ot_ready, 1)

                body(0, True, False, False)
                body(1, True, True, False)
                with act.Fori(2, STEPS - 1) as i:
                    body(i, True, True, True)
                body(STEPS - 1, True, True, True)
                body(STEPS, False, True, True)
                body(STEPS + 1, False, False, True)

            part(0)
            stack(0)
            part(1)
            stack(1)
            for g in range(4):
                act.wait_ge(o_t, g + 1)
                sca.activation(XL[:, g, :], TB[g % 2], ACT.Copy).then_inc(o_ready, 1)

        @block.gpsimd
        def _(pool):
            gp = nc.gpsimd

            def part_init(p):
                if p == 1:
                    pool.wait_ge(y_ready, B + STEPS)
                gp.memset(KS[:, :, :], 1.0)
                gp.memset(QS[:, :, :], 0.0).then_inc(va_clear, 1)
                gp.memset(VA[:, :, :, 0:DH], 0.0)
                gp.memset(VA[:, :, :, DH + 1:32], 0.0)
                gp.memset(VA[:, :, :, DH:DH + 1], 1.0).then_inc(va_clear, 1)

            def stack(ph):
                pool.wait_ge(y_ready, (B + STEPS) * ph + B)

                def table(m, layer):
                    gp.tensor_tensor(out=TAB[:, m, :, :].rearrange("p (q c) f -> p q c f", q=2),
                                     in0=ROT[:, m, :, :].rearrange("p (q c) f -> p q c f", q=2),
                                     in1=QSC[:, layer, :, :].unsqueeze(2).broadcast_to([128, 2, 2, LD]),
                                     op=ALU.mult).then_inc(tab_ready, 1)
                for m in range(BLK - 1):
                    table(m, 0)

                def body(i, cur, prev, prev2):
                    for n in range(BLK):
                        G = BLK * STEPS * ph + BLK * i + n
                        J = STEPS * ph + i - 1
                        J2 = J - 1
                        def vectors():
                            if prev and n == 0:
                                gp.tensor_copy(PARN[:, :], PARL[:, (i - 1) // B, :]).then_inc(parn_ready, 1)
                            if prev and n == 3:
                                gp.tensor_copy(PARF[:, :], PARL[:, (i - 1) // B, :]).then_inc(parf_ready, 1)

                        if prev2 and n == 0:
                            pool.wait_ge(h_ready, FT * J2 + 1)
                        if prev and prev2 and n == 3:
                            pool.wait_ge(y_ready, (B + STEPS) * ph + i + 3)
                        if not cur:
                            vectors()
                            continue
                        for j in range(4):
                            u = 4 * G + j
                            pool.wait_ge(rot_mul, 2 * (u + 1))
                            pool.wait_ge(b_mm, seen(u - 3))
                            gp.tensor_tensor(out=QN[:, j, :], in0=T1[:, j % 2, :], in1=T2[:, j % 2, :], op=ALU.add)\
                              .then_inc(rot_add, 1)
                            if j == 0:
                                vectors()
                                if n == 0:
                                    table(BLK - 1, i // B)
                                else:
                                    table(n - 1, ((i + 1) // B) % LAYERS)
                        pool.wait_ge(rn_step, RN * (G + 1))
                        pool.wait_ge(rot_add, 4 * G + 4)
                        for j in range(2, 4):
                            v = QN[:, j, :].rearrange("p (h f) -> p h f", f=LD)
                            gp.tensor_tensor(out=v, in0=v, in1=SY[:, 8 * j:8 * j + 8].unsqueeze(2)
                                             .broadcast_to([128, 8, LD]), op=ALU.mult).then_inc(k_norm, 1)

                body(0, True, False, False)
                body(1, True, True, False)
                with pool.Fori(2, STEPS) as i:
                    body(i, True, True, True)
                body(STEPS, False, True, True)
                body(STEPS + 1, False, False, True)

            gp.memset(PARL[:, :, :], 0.0).then_inc(parl_clear, 1)
            part_init(0)
            pool.wait_ge(vecs_loaded, 16 * VEC_LOADS)
            pool.wait_ge(con_loaded, 16)
            stack(0)
            part_init(1)
            stack(1)

        @block.sync
        def _(sp):
            sp.dma_start(CON[:, :], a["consts"]).then_inc(con_loaded, 16)
            sp.dma_start(XL[:, :, :].rearrange("p g (m f) -> p (g m) f", f=D),
                         a["L0_attn_a_x"].rearrange("b t f -> (b t) f").rearrange("(n p) f -> p n f", p=128))\
              .then_inc(x_loaded, 16)
            for z, name in enumerate(("Wq", "Wk", "Wv")):
                sp.dma_start(WA[:, z, :], a["L0_attn_a_" + name]).then_inc(mats_loaded, 16)
                sp.dma_start(WB[:, z, :], a["L0_attn_b_" + name]).then_inc(mats_loaded, 16)

            def col(ap):
                return ap.rearrange("(p o) -> p o", o=1)

            def load_layer(L, layer):
                sp.dma_start(W[:, L % 2, :], a["L0_ffn_Wqkv"][layer, :, :]).then_inc(wqkv_loaded, 16)

            def load_wo(layer):
                wo = a["L0_ffn_Wo"][layer, :, :].rearrange("(h p) m -> p h m", p=128)
                sp.dma_start(WO[:, 0, :, :], wo).then_inc(wo_loaded, 16)
                sp.dma_start(WO[0:64, 1, :, :], wo[64:128]).then_inc(wo_loaded, 16)
                sp.dma_start(WO[64:128, 1, :, :], wo[0:64]).then_inc(wo_loaded, 16)

            def load_w1(layer):
                sp.dma_start(W1[:, :], a["L0_ffn_W1"][layer, :, :]).then_inc(w1_loaded, 16)

            def load_w2(layer):
                w2 = a["L0_ffn_W2"][layer, :, :]
                full = 128 * (FT - 1)
                sp.dma_start(W2[:, 0:FT - 1, :], w2[0:full, :].rearrange("(t p) m -> p t m", p=128))\
                  .then_inc(w2_loaded, 16)
                sp.dma_start(W2[0:FR[-1], FT - 1, :], w2[full:FF, :]).then_inc(w2_loaded, 16)

            with nc.allow_non_contiguous_dma(reason="vectors by partition, once"):
                for z, name in enumerate(("bq", "bk", "ln_g", "ln_b")):
                    sp.dma_start(VEC[:, z:z + 1], col(a["L0_attn_a_" + name])).then_inc(vecs_loaded, 16)
                sp.dma_start(BVB[:, :], a["L0_attn_a_bv"].rearrange("(o f) -> o f", o=1).broadcast_to([128, 128]))\
                  .then_inc(vecs_loaded, 16)
                sp.wait_ge(parl_clear, 1)
                for t in range(FT):
                    r = FR[t]
                    for c0, o in ((P_B1A, 0), (P_B1G, FF)):
                        sp.dma_start(PARL[0:r, :, c0 + t],
                                     a["L0_ffn_b1"][:, o + 128 * t:o + 128 * t + r].rearrange("l p -> p l"))\
                          .then_inc(vecs_loaded, 16)
                for c0, name in ((P_B2, "b2"), (P_G, "ln_g"), (P_B, "ln_b")):
                    sp.dma_start(PARL[:, :, c0], a["L0_ffn_" + name].rearrange("l p -> p l"))\
                      .then_inc(vecs_loaded, 16)
                for z, name in enumerate(("q_scale", "k_scale")):
                    src = a["L0_ffn_" + name].rearrange("(o l) f -> o l f", o=1).broadcast_to([128, LAYERS, LD])
                    sp.dma_start(QSC[:, :, z, :], src).then_inc(vecs_loaded, 16)
            load_layer(0, 0)
            load_layer(1, 1)
            load_wo(0)
            load_w1(0)
            load_w2(0)

            def part(p):
                def body(b):
                    c = B * p + b
                    sp.wait_ge(parts_ready, 2 * c + 2)
                    sp.dma_start(scr_parts.rearrange("k p t -> p k t"), PTS[:, :, :]).then_inc(scr_written, 16)
                    sp.wait_ge(scr_written, 16 * (c + 1))
                    sp.wait_ge(va_clear, 2 * p + 1)
                    for r in range(len(Q_PARTS)):
                        for z, (dst, src) in enumerate(((QS, Q_PARTS), (KS, K_PARTS))):
                            rows = dst[DH * r:DH * r + DH, :, :] if p == 0 else \
                                STG[64 * z + DH * r:64 * z + DH * r + DH, :, :]
                            sp.dma_start(rows,
                                         scr_parts[PARTS * z + src[r], :, :].rearrange("(h d) t -> d h t", d=DH))\
                              .then_inc(qs_loaded, 16)
                    for g in range(4):
                        sp.wait_ge(mt_ready, 4 * c + g + 1)
                        quarter = scr_max[:, 16 * g:16 * g + 16, :]
                        sp.dma_start(quarter.rearrange("k u q -> u k q"), MT[:, :, :]).then_inc(m_written, 16)
                        sp.wait_ge(m_written, 16 * (4 * c + g + 1))
                        sp.dma_start(QS[MROW:MROW + PARTS, 4 * g:4 * g + 4, :],
                                     quarter.rearrange("k (h q) t -> k h (q t)", h=4)).then_inc(m_loaded, 16)
                    if p == 1:
                        sp.wait_ge(att_out, b + 1)
                        sp.dma_start(scr_att, OS[:, 0, :]).then_inc(att_written, 16)
                        sp.wait_ge(att_written, 16 * (b + 1))
                        for cc in range(T // 32):
                            sp.dma_start(ATT[DH * cc:DH * cc + DH, :, :].rearrange("p m (h t) -> p (m h) t", t=32),
                                         scr_att[:, 32 * cc:32 * cc + 32].rearrange("(h d) t -> d h t", d=DH))\
                              .then_inc(att_loaded, 16)
                part_loop(sp, body)

            def stack(ph):
                def shift(g, z):
                    sp.wait_ge(v_ready, 2 * g + 2)
                    for v, to, frm, rows, before in V_COPIES:
                        sp.dma_start(VT[to:to + rows, z, v + 1, :],
                                     VT[frm:frm + rows, 1 - z if before else z, v, :]).then_inc(v_shifted, 16)

                def next_wo(L, layer):
                    sp.wait_ge(wo_mm, B * L)
                    load_wo(layer)

                def next_w1(L, layer):
                    sp.wait_ge(a_mm, FT * B * L)
                    load_w1(layer)

                def next_w2(L, layer):
                    sp.wait_ge(w2_mm, B * L)
                    load_w2(layer)

                def body(layer, first, qkv):
                    L = LAYERS * ph + layer
                    g0 = BLK * B * L
                    for n in range(2 * BLK):
                        shift(g0 + n, n % 2)
                        if n == 0 and not first:
                            next_wo(L, layer)
                        if n == BLK and not first:
                            next_w1(L, layer)
                        if n == BLK + 2 and not first:
                            next_w2(L, layer)
                    with sp.Fori(BLK, BLK * B // 2) as pair:
                        for z in range(2):
                            shift(g0 + 2 * pair + z, z)
                    if qkv:
                        sp.wait_ge(v_mm, 2 * BLK * B * (L + 1))
                        load_layer(layer, (layer + 2) % LAYERS)

                body(0, True, True)
                if ph == 0:
                    with sp.Fori(1, LAYERS) as layer:
                        body(layer, False, True)
                    next_wo(LAYERS, 0)
                    next_w1(LAYERS, 0)
                    next_w2(LAYERS, 0)
                else:
                    with sp.Fori(1, LAYERS - 2) as layer:
                        body(layer, False, True)
                    with sp.Fori(LAYERS - 2, LAYERS) as layer:
                        body(layer, False, False)

            part(0)
            stack(0)
            part(1)
            stack(1)
            for g in range(4):
                sp.wait_ge(o_ready, g + 2)
                sp.dma_start(out[g, :, :].rearrange("(m p) f -> p m f", p=128),
                             XL[:, g, :].rearrange("p (m f) -> p m f", f=D)).then_inc(o_stored, 16)
            sp.wait_ge(o_stored, 64)


_INS = ['L0_attn_a_x', 'L0_attn_a_ln_g', 'L0_attn_a_ln_b', 'L0_attn_a_Wq', 'L0_attn_a_bq', 'L0_attn_a_Wk',
        'L0_attn_a_bk', 'L0_attn_a_Wv', 'L0_attn_a_bv', 'L0_attn_b_Wq', 'L0_attn_b_Wk', 'L0_attn_b_Wv',
        'L0_ffn_Wqkv', 'L0_ffn_q_scale', 'L0_ffn_k_scale', 'L0_ffn_Wo', 'L0_ffn_ln_g', 'L0_ffn_ln_b',
        'L0_ffn_W1', 'L0_ffn_b1', 'L0_ffn_W2', 'L0_ffn_b2']


def kernel(**inputs):
    import numpy as _np
    import concourse.bacc as _bacc
    from concourse import mybir as _mybir
    from concourse.bass_utils import run_bass_kernel_spmd as _run

    nc = _bacc.Bacc("TRN2", target_bir_lowering=False, num_devices=1)
    arrays = {f"in_{n}_dram": _np.ascontiguousarray(inputs[n]) for n in _INS}
    arrays["in_consts_dram"] = host_constants()
    aps = {n: nc.dram_tensor(f"in_{n}_dram", arrays[f"in_{n}_dram"].shape,
                             _mybir.dt.from_np(arrays[f"in_{n}_dram"].dtype), kind="ExternalInput").ap()
           for n in [*_INS, "consts"]}
    out = nc.dram_tensor("out_0_dram", (B, T, D), F32, kind="ExternalOutput").ap()
    scr_parts = nc.dram_tensor("scr_parts", (2 * PARTS, 128, T), BF16).ap()
    scr_max = nc.dram_tensor("scr_max", (PARTS, 64, 128), BF16).ap()
    scr_att = nc.dram_tensor("scr_att", (128, T), F32).ap()
    hybrid_kernel(nc, aps, out, scr_parts, scr_max, scr_att)
    r = _run(nc, [arrays], core_ids=[0])
    return r.results[0]["out_0_dram"]
```
